# Optimizing a Trainium2 kernel written in Bass

```python
import numpy as np
import jax
import jax.numpy as jnp

def _softmax(x, axis=-1):
    return jax.nn.softmax(x, axis=axis)

def _gelu(x):
    return jax.nn.gelu(x, approximate=True)

def _silu(x):
    return jax.nn.silu(x)

def _sigmoid(x):
    return jax.nn.sigmoid(x)

def _layernorm(x, axis=-1, eps=1e-05):
    m = jnp.mean(x, axis=axis, keepdims=True)
    v = jnp.var(x, axis=axis, keepdims=True)
    return (x - m) / jnp.sqrt(v + eps)

def _scatter_add(tgt, idx, src, axis=0):
    return tgt.at[idx].add(src)

def _segment_sum(src, seg, n):
    return jax.ops.segment_sum(src, seg, n)
kernel_name = 'mk_xattn_seq_d2_seqx_r4_f3fdea'

def setup_inputs(seed: int=0):
    np.random.seed(seed)
    _w = jnp.asarray

    def _rec_inputs():
        import jax
        import jax.numpy as jnp
        _rk = jax.random.key(seed)
        x = -0.0005207 + 1.001 * jax.random.normal(jax.random.fold_in(_rk, 1), (16, 256, 256), jnp.float32)
        _lenS = 256 - jax.random.randint(jax.random.fold_in(_rk, 7), (16,), 0, max(1, 256 // 4) + 1, jnp.int32)
        _lenS2 = 77 - jax.random.randint(jax.random.fold_in(_rk, 8), (16,), 0, max(1, 77 // 4) + 1, jnp.int32)
        _ctx_1024P = jax.random.normal(jax.random.fold_in(_rk, 11), (16, 16, 256), jnp.float32)
        _ctx_1024c = jax.random.dirichlet(jax.random.fold_in(_rk, 511), 0.3 * jnp.ones((16,), jnp.float32), (16, 77))
        _ctx_1024t = jnp.einsum('bsk,bkd->bsd', _ctx_1024c, _ctx_1024P)
        _ctx_1024t = _ctx_1024t * jax.lax.rsqrt(jnp.mean(jnp.square(_ctx_1024t)) + 1e-12) * 0.953939
        ctx_1024 = -0.000514642 + 1.00011 * (_ctx_1024t + 0.3 * jax.random.normal(jax.random.fold_in(_rk, 611), (16, 77, 256), jnp.float32))
        return (x, ctx_1024)
    x, ctx_1024 = _rec_inputs()

    def _L0_xattn_setup():
        import jax, jax.numpy as jnp
        import numpy as np
        H = 256
        NH = 16
        HD = H // NH
        I = 1024
        EPS = 1e-06

        def rmsnorm(x, w, eps=EPS):
            var = jnp.mean(jnp.square(x), axis=-1, keepdims=True)
            return x * jax.lax.rsqrt(var + eps) * w

        def attention(x, ctx, wq, wk, wv, wo):
            B, S, _ = x.shape
            Skv = ctx.shape[1]
            q = (x @ wq).reshape(B, S, NH, HD)
            k = (ctx @ wk).reshape(B, Skv, NH, HD)
            v = (ctx @ wv).reshape(B, Skv, NH, HD)
            scores = jnp.einsum('bqhd,bkhd->bhqk', q, k) * HD ** (-0.5)
            attn = jax.nn.softmax(scores.astype(jnp.float32), axis=-1).astype(q.dtype)
            out = jnp.einsum('bhqk,bkhd->bqhd', attn, v).reshape(B, S, NH * HD)
            return out @ wo

        def mlp(x, wg, wu, wd):
            return jax.nn.silu(x @ wg) * (x @ wu) @ wd
        key = jax.random.key(seed)
        ks = jax.random.split(key, 16)
        p = lambda k, shape: jax.random.normal(k, shape, jnp.float32) * 0.02
        return {'hidden_states': jax.random.normal(ks[0], (1, 512, H), jnp.float32), 'context': jax.random.normal(ks[1], (1, 512, H), jnp.float32), 'sa_norm_w': jnp.ones((H,), jnp.float32), 'sa_wq': p(ks[2], (H, NH * HD)), 'sa_wk': p(ks[3], (H, NH * HD)), 'sa_wv': p(ks[4], (H, NH * HD)), 'sa_wo': p(ks[5], (NH * HD, H)), 'ca_norm_w': jnp.ones((H,), jnp.float32), 'ca_wq': p(ks[6], (H, NH * HD)), 'ca_wk': p(ks[7], (H, NH * HD)), 'ca_wv': p(ks[8], (H, NH * HD)), 'ca_wo': p(ks[9], (NH * HD, H)), 'mlp_norm_w': jnp.ones((H,), jnp.float32), 'w_gate': p(ks[10], (H, I)), 'w_up': p(ks[11], (H, I)), 'w_down': p(ks[12], (I, H))}
    _L0_xattn_all = _L0_xattn_setup()
    _L0_xattn_in = {k: v for k, v in _L0_xattn_all.items() if k in ('sa_norm_w', 'sa_wq', 'sa_wk', 'sa_wv', 'sa_wo', 'ca_norm_w', 'ca_wq', 'ca_wk', 'ca_wv', 'ca_wo', 'mlp_norm_w', 'w_gate', 'w_up', 'w_down')}
    del _L0_xattn_all

    def _L1_xattn_setup():
        import jax, jax.numpy as jnp
        import numpy as np
        EMBED_DIM = 256
        LN_EPS = 1e-05

        def _layernorm(x, w, b):
            m = jnp.mean(x, axis=-1, keepdims=True)
            v = jnp.mean(jnp.square(x - m), axis=-1, keepdims=True)
            return (x - m) * jax.lax.rsqrt(v + LN_EPS) * w + b

        def _attention(q, k, v, scale):
            scores = jnp.einsum('bqd,bkd->bqk', q, k) * scale
            probs = jax.nn.softmax(scores, axis=-1)
            return jnp.einsum('bqk,bkd->bqd', probs, v)
        key = jax.random.key(seed)
        ks = jax.random.split(key, 16)
        B, SQ, SK, D, H = (8, 577, 13271, EMBED_DIM, 4)
        return {'input_features': jax.random.normal(ks[0], (B, SK, D), jnp.float32), 'query_feature': jax.random.normal(ks[1], (B, SQ, D), jnp.float32), 'norm1_w': jax.random.uniform(ks[2], (D,), jnp.float32, 0.5, 1.5), 'norm1_b': jax.random.normal(ks[3], (D,), jnp.float32) * 0.1, 'norm2_w': jax.random.uniform(ks[4], (D,), jnp.float32, 0.5, 1.5), 'norm2_b': jax.random.normal(ks[5], (D,), jnp.float32) * 0.1, 'norm3_w': jax.random.uniform(ks[6], (D,), jnp.float32, 0.5, 1.5), 'norm3_b': jax.random.normal(ks[7], (D,), jnp.float32) * 0.1, 'gamma1': jax.random.uniform(ks[8], (D,), jnp.float32, 0.5, 1.5), 'gamma2': jax.random.uniform(ks[9], (D,), jnp.float32, 0.5, 1.5), 'fc1_w': jax.random.normal(ks[10], (H, D), jnp.float32) * (1.0 / np.sqrt(D)), 'fc1_b': jax.random.normal(ks[11], (H,), jnp.float32) * 0.01, 'fc2_w': jax.random.normal(ks[12], (D, H), jnp.float32) * (1.0 / np.sqrt(H)), 'fc2_b': jax.random.normal(ks[13], (D,), jnp.float32) * 0.01}
    _L1_xattn_all = _L1_xattn_setup()
    _L1_xattn_in = {k: v for k, v in _L1_xattn_all.items() if k in ('norm1_w', 'norm1_b', 'norm2_w', 'norm2_b', 'norm3_w', 'norm3_b', 'gamma1', 'gamma2', 'fc1_w', 'fc1_b', 'fc2_w', 'fc2_b')}
    del _L1_xattn_all
    return {'x': x, 'ctx_1024': ctx_1024, 'L0_xattn_sa_norm_w': _L0_xattn_in['sa_norm_w'], 'L0_xattn_sa_wq': _L0_xattn_in['sa_wq'], 'L0_xattn_sa_wk': _L0_xattn_in['sa_wk'], 'L0_xattn_sa_wv': _L0_xattn_in['sa_wv'], 'L0_xattn_sa_wo': _L0_xattn_in['sa_wo'], 'L0_xattn_ca_norm_w': _L0_xattn_in['ca_norm_w'], 'L0_xattn_ca_wq': _L0_xattn_in['ca_wq'], 'L0_xattn_ca_wk': _L0_xattn_in['ca_wk'], 'L0_xattn_ca_wv': _L0_xattn_in['ca_wv'], 'L0_xattn_ca_wo': _L0_xattn_in['ca_wo'], 'L0_xattn_mlp_norm_w': _L0_xattn_in['mlp_norm_w'], 'L0_xattn_w_gate': _L0_xattn_in['w_gate'], 'L0_xattn_w_up': _L0_xattn_in['w_up'], 'L0_xattn_w_down': _L0_xattn_in['w_down'], 'L1_xattn_norm1_w': _L1_xattn_in['norm1_w'], 'L1_xattn_norm1_b': _L1_xattn_in['norm1_b'], 'L1_xattn_norm2_w': _L1_xattn_in['norm2_w'], 'L1_xattn_norm2_b': _L1_xattn_in['norm2_b'], 'L1_xattn_norm3_w': _L1_xattn_in['norm3_w'], 'L1_xattn_norm3_b': _L1_xattn_in['norm3_b'], 'L1_xattn_gamma1': _L1_xattn_in['gamma1'], 'L1_xattn_gamma2': _L1_xattn_in['gamma2'], 'L1_xattn_fc1_w': _L1_xattn_in['fc1_w'], 'L1_xattn_fc1_b': _L1_xattn_in['fc1_b'], 'L1_xattn_fc2_w': _L1_xattn_in['fc2_w'], 'L1_xattn_fc2_b': _L1_xattn_in['fc2_b']}

def reference(x, ctx_1024, L0_xattn_sa_norm_w, L0_xattn_sa_wq, L0_xattn_sa_wk, L0_xattn_sa_wv, L0_xattn_sa_wo, L0_xattn_ca_norm_w, L0_xattn_ca_wq, L0_xattn_ca_wk, L0_xattn_ca_wv, L0_xattn_ca_wo, L0_xattn_mlp_norm_w, L0_xattn_w_gate, L0_xattn_w_up, L0_xattn_w_down, L1_xattn_norm1_w, L1_xattn_norm1_b, L1_xattn_norm2_w, L1_xattn_norm2_b, L1_xattn_norm3_w, L1_xattn_norm3_b, L1_xattn_gamma1, L1_xattn_gamma2, L1_xattn_fc1_w, L1_xattn_fc1_b, L1_xattn_fc2_w, L1_xattn_fc2_b):
    import jax
    import jax.numpy as jnp

    def _L0_xattn_ref(hidden_states, context, sa_norm_w, sa_wq, sa_wk, sa_wv, sa_wo, ca_norm_w, ca_wq, ca_wk, ca_wv, ca_wo, mlp_norm_w, w_gate, w_up, w_down):
        import jax, jax.numpy as jnp
        import numpy as np
        H = 256
        NH = 16
        HD = H // NH
        I = 1024
        EPS = 1e-06

        def rmsnorm(x, w, eps=EPS):
            var = jnp.mean(jnp.square(x), axis=-1, keepdims=True)
            return x * jax.lax.rsqrt(var + eps) * w

        def attention(x, ctx, wq, wk, wv, wo):
            B, S, _ = x.shape
            Skv = ctx.shape[1]
            q = (x @ wq).reshape(B, S, NH, HD)
            k = (ctx @ wk).reshape(B, Skv, NH, HD)
            v = (ctx @ wv).reshape(B, Skv, NH, HD)
            scores = jnp.einsum('bqhd,bkhd->bhqk', q, k) * HD ** (-0.5)
            attn = jax.nn.softmax(scores.astype(jnp.float32), axis=-1).astype(q.dtype)
            out = jnp.einsum('bhqk,bkhd->bqhd', attn, v).reshape(B, S, NH * HD)
            return out @ wo

        def mlp(x, wg, wu, wd):
            return jax.nn.silu(x @ wg) * (x @ wu) @ wd
        residual = hidden_states
        h = rmsnorm(hidden_states, sa_norm_w)
        h = residual + attention(h, h, sa_wq, sa_wk, sa_wv, sa_wo)
        residual = h
        hn = rmsnorm(h, ca_norm_w)
        h = residual + attention(hn, context, ca_wq, ca_wk, ca_wv, ca_wo)
        residual = h
        hn = rmsnorm(h, mlp_norm_w)
        h = residual + mlp(hn, w_gate, w_up, w_down)
        return h

    def _L1_xattn_ref(input_features, query_feature, norm1_w, norm1_b, norm2_w, norm2_b, norm3_w, norm3_b, gamma1, gamma2, fc1_w, fc1_b, fc2_w, fc2_b):
        import jax, jax.numpy as jnp
        import numpy as np
        EMBED_DIM = 256
        LN_EPS = 1e-05

        def _layernorm(x, w, b):
            m = jnp.mean(x, axis=-1, keepdims=True)
            v = jnp.mean(jnp.square(x - m), axis=-1, keepdims=True)
            return (x - m) * jax.lax.rsqrt(v + LN_EPS) * w + b

        def _attention(q, k, v, scale):
            scores = jnp.einsum('bqd,bkd->bqk', q, k) * scale
            probs = jax.nn.softmax(scores, axis=-1)
            return jnp.einsum('bqk,bkd->bqd', probs, v)
        scale = EMBED_DIM ** (-0.5)
        norm_X = _layernorm(input_features, norm1_w, norm1_b)
        norm_F_L = _layernorm(query_feature, norm2_w, norm2_b)
        attended = _attention(norm_F_L, norm_X, norm_X, scale)
        h = jax.nn.gelu(attended @ fc1_w.T + fc1_b, approximate=False)
        cross_attended = h @ fc2_w.T + fc2_b
        norm_cross = _layernorm(cross_attended, norm3_w, norm3_b)
        self_attended = _attention(norm_cross, norm_cross, norm_cross, scale)
        skip_connect = cross_attended + gamma1 * self_attended
        return norm_F_L + gamma2 * skip_connect
    x = _L0_xattn_ref(x, ctx_1024, L0_xattn_sa_norm_w, L0_xattn_sa_wq, L0_xattn_sa_wk, L0_xattn_sa_wv, L0_xattn_sa_wo, L0_xattn_ca_norm_w, L0_xattn_ca_wq, L0_xattn_ca_wk, L0_xattn_ca_wv, L0_xattn_ca_wo, L0_xattn_mlp_norm_w, L0_xattn_w_gate, L0_xattn_w_up, L0_xattn_w_down)
    x = _L1_xattn_ref(ctx_1024, x, L1_xattn_norm1_w, L1_xattn_norm1_b, L1_xattn_norm2_w, L1_xattn_norm2_b, L1_xattn_norm3_w, L1_xattn_norm3_b, L1_xattn_gamma1, L1_xattn_gamma2, L1_xattn_fc1_w, L1_xattn_fc1_b, L1_xattn_fc2_w, L1_xattn_fc2_b)
    return x

_drawn_inputs = setup_inputs


def setup_inputs(seed=0):
    import zlib

    import numpy as np

    out = dict(_drawn_inputs(seed))
    spreads = {'L0_xattn_sa_norm_w': (1.0, 0.6),
     'L0_xattn_ca_norm_w': (1.0, 0.6),
     'L0_xattn_mlp_norm_w': (1.0, 0.6)}
    factors = {'L0_xattn_sa_wq': 8.0,
     'L0_xattn_sa_wk': 8.0,
     'L0_xattn_sa_wv': 8.0,
     'L0_xattn_sa_wo': 8.0,
     'L0_xattn_ca_wq': 57.706,
     'L0_xattn_ca_wk': 56.788,
     'L1_xattn_fc1_b': 4.378,
     'L0_xattn_ca_wv': 5.867,
     'L0_xattn_ca_wo': 6.182,
     'L0_xattn_w_gate': 8.0,
     'L0_xattn_w_up': 8.0,
     'L0_xattn_w_down': 8.0}
    for name, (base, spread) in spreads.items():
        noise = np.random.default_rng([zlib.crc32(name.encode()), seed]).standard_normal(out[name].shape)
        drawn = base * np.exp(spread * noise) if base else spread * noise
        out[name] = jnp.asarray(drawn.astype(out[name].dtype))
    for name, factor in factors.items():
        out[name] = (out[name] * factor).astype(out[name].dtype)
    return out
```

```python
from contextlib import ExitStack

import concourse.bass as bass
from concourse import mybir

F32 = mybir.dt.float32
F32R = mybir.dt.float32r
ALU = mybir.AluOpType
ACT = mybir.ActivationFunctionType
AX_X = mybir.AxisListType.X

P = 128
B, T, D = 16, 256, 256
SKV = 77
SKV2 = SKV + 1
NH, HD = 16, 16
INNER = 1024
FC = 4
C = D // P
QT = T // P
M = INNER // P
PAIRS = 4
RMS_EPS = 1e-6
LN_EPS = 1e-5
HEAD_SCALE = HD ** -0.5
L1_SCALE = D ** -0.5
PARTS = ((0, 0), (0, 1), (1, 0))

ATTN_W = ["sa_wq", "sa_wk", "sa_wv", "sa_wo", "ca_wq", "ca_wk", "ca_wv", "ca_wo"]
ROWS = ["n1w", "n1b", "n2w", "n2b", "n3w", "n3b", "g1", "g2"]

PREPARE = ("norm", "xn", "T", "qk", "v", "pack")
ITERATION = [
    ("norm", "mlp"), ("S", "sa", 0), ("xn", "mlp"), ("S", "sa", 1), ("T", "mlp"), ("S", "sa", 2), ("S", "sa", 3), ("maxsplit", "sa", 0),
    ("gu", 0), ("S", "sa", 4), ("maxT", "sa", 0), ("gu", 1), ("S", "sa", 5), ("gu", 2), ("S", "sa", 6), ("gu", 3),
    ("S", "sa", 7), ("maxsplit", "sa", 1), ("gu", 4),
    ("E", "sa", 0), ("maxT", "sa", 1), ("gu", 5), ("E", "sa", 1), ("E", "sa", 2), ("gu", 6), ("pv", "sa", 0), ("E", "sa", 3), ("E", "sa", 4), ("gu", 7),
    ("pv", "sa", 1), ("at", "sa", 0), ("lnstat", "nx"), ("E", "sa", 5), ("E", "sa", 6), ("pv", "sa", 2), ("lncen", "nx"), ("E", "sa", 7),
    ("nXT",), ("pv", "sa", 3), ("at", "sa", 1), ("dn",), ("wo", "sa"),
    ("norm", "ca"), ("lnstat", "nf"), ("cT", "ca"), ("xn", "ca"), ("T", "ca"), ("lncen", "nf"), ("qk", "ca"), ("nFT",), ("v", "ca"),
    ("sc",), ("pack", "ca", 0), ("norm", "sa"), ("pack", "ca", 1), ("pT",), ("xn", "sa"),
    ("S", "ca", 0), ("S", "ca", 1), ("maxsplit", "ca", 0), ("h4",), ("S", "ca", 2), ("maxT", "ca", 0), ("S", "ca", 3), ("maxsplit", "ca", 1),
    ("f2",), ("T", "sa"), ("E", "ca", 0), ("maxT", "ca", 1), ("E", "ca", 1), ("lnstat", "nc"), ("qk", "sa"), ("E", "ca", 2), ("pv", "ca", 0), ("lncen", "nc"),
    ("at", "ca", 0), ("E", "ca", 3), ("nCT",), ("pv", "ca", 1), ("at", "ca", 1), ("v", "sa"), ("s2",), ("pack", "sa", 0),
    ("wo", "ca"), ("p2T",), ("pack", "sa", 1), ("pv2",), ("out",),
]


def track(step):
    if step[-1] == "mlp" or step[0] in ("gu", "dn", "lnstat", "lncen", "out", "nFT", "nXT", "sc", "pT", "h4", "f2", "nCT", "s2", "p2T", "pv2"):
        return -1
    return 1 if step[0] in PREPARE and step[1] == "sa" else 0


def fills_of(step):
    if step[0] == "T" and step[1] == "mlp":
        return [], ["mT"]
    if step[0] in ("T", "qk", "v", "wo", "cT"):
        return [(step[1], step[0])], []
    if step[0] in ("S", "E"):
        return [(step[1], step[0], step[2])], []
    if step[0] == "pack":
        _, tag, c = step
        return [(tag, "pq", c)] + ([(tag, "pk", c)] if tag == "sa" or c == 0 else []), []
    if step[0] == "gu":
        return [], [f"gu{step[1]}"]
    return [], [step[0]] if step[0] in ("dn", "nFT", "nXT", "sc", "pT", "h4", "f2", "nCT", "s2", "p2T", "pv2") else []


A_FILLS = [f for step in ITERATION for f in fills_of(step)[0]]
M_FILLS = [f for step in ITERATION for f in fills_of(step)[1]]
A_AHEAD = [track(step) for step in ITERATION for f in fills_of(step)[0]]


class Signal:

    def __init__(self, sem, per):
        self.sem, self.per = sem, per

    def at(self, n, j):
        return n * self.per + j


def not_first(n):
    return not isinstance(n, int) or n > 0


def build(nc, x, ctx, w, vecs, norm_w, fc1t, fc1b, fc2t, fc2b, out):
    st = ExitStack()
    with st:
        def sb(name, shape, dt=F32):
            return st.enter_context(nc.sbuf_tensor(name, shape, dt))

        def sem(name):
            return st.enter_context(nc.semaphore(name))

        def sig(name, per):
            return Signal(sem(name), per)

        wt = {n: [sb(f"{n}_{p}", [P, C, D], F32R) for p in ("hi", "lo")] for n in ATTN_W}
        for n in ("gate", "up"):
            wt[n] = [sb(f"{n}_{p}", [P, C, INNER], F32R) for p in ("hi", "lo")]
        wt["down"] = [sb(f"down_{p}", [P, M, D], F32R) for p in ("hi", "lo")]
        W_ORDER = ATTN_W + ["gate", "up", "down"]
        normw = sb("normw", [P, 3, C])
        NORM_AT = {"sa": 0, "ca": 1, "mlp": 2}
        bc = sb("bc", [P, len(ROWS), D])
        fc1t_sb = sb("fc1t_sb", [P, C, FC])
        fc1b_sb = sb("fc1b_sb", [FC, 1])
        fc2_sb = sb("fc2_sb", [FC + 1, D])
        ident = sb("ident", [P, P])
        ones_row = sb("ones_row", [1, P])
        half_neg = sb("half_neg", [P, QT])
        ones_pad = sb("ones_pad", [P, 2, 32])
        sel = sb("sel", [P, 4, PAIRS, P], F32R)
        maxsel = sb("maxsel", [P, 8, 2], F32R)
        x_sb = sb("x_sb", [P, QT, D])
        ctx_sb = sb("ctx_sb", [SKV, D])
        h1 = sb("h1", [P, QT, D])
        h2 = sb("h2", [P, QT, D])
        ss = {t: sb(f"{t}_sumsq", [P, QT]) for t in NORM_AT}
        ms = {t: sb(f"{t}_meansq", [P, QT]) for t in NORM_AT}
        rstd = {t: sb(f"{t}_rstd", [P, QT]) for t in NORM_AT}
        xn_a = sb("xn_a", [P, QT, D])
        xn_m = sb("xn_m", [P, QT, D])
        hT_a = [sb(f"hT_a_{p}", [P, C, T], F32R) for p in ("hi", "lo")]
        hT_m = [sb(f"hT_m_{p}", [P, C, T], F32R) for p in ("hi", "lo")]
        cT = [sb(f"cT_{p}", [P, C, SKV2], F32R) for p in ("hi", "lo")]
        qT = [sb(f"qT_{p}", [P, C, T], F32R) for p in ("hi", "lo")]
        kT = [sb(f"kT_{p}", [P, C, T], F32R) for p in ("hi", "lo")]
        qpk = sb("qpk", [P, 2 * PAIRS, T], F32R)
        kpk = sb("kpk", [P, 2 * PAIRS, T], F32R)
        vz = sb("vz", [P, QT, NH, 32])
        GRANULES = 2
        probs = sb("probs", [P, GRANULES, PAIRS, 2, T])
        mx = sb("mx", [P, C, QT, 8])
        nm = sb("nm", [P, C, QT, 80])
        negT = sb("negT", [P, C, T], F32R)
        rD = sb("rD", [P, T])
        at = xn_a
        atT = [sb(f"atT_{p}", [P, C, T], F32R) for p in ("hi", "lo")]
        hid = sb("hid", [P, 2, T])
        hidT = [sb(f"hidT_{p}", [P, M, T], F32R) for p in ("hi", "lo")]
        ctx_l = sb("ctx_l", [SKV, 1, D])
        buf = [sb(f"l1_buf{i}", [P, QT, D]) for i in range(5)]
        h3 = cross = buf[0]
        nF, nC, sp2 = buf[1], buf[2], buf[3]
        t1 = buf[3]
        nFT = nCT = p2T = buf[4]
        o_sb = sb("o_sb", [P, QT, D])
        row_of = lambda k: buf[k // QT][0:1, k % QT, :]
        LN = {"nf": (P, QT, 2), "nx": (SKV, 1, 0), "nc": (P, QT, 4)}
        NRM = {"nf": nF, "nx": ctx_l, "nc": nC}
        stats = {t: sb(f"{t}_stats", [r, q, 6]) for t, (r, q, _) in LN.items()}
        mv = {t: sb(f"{t}_mv", [r, q, 2]) for t, (r, q, _) in LN.items()}
        ve = {t: sb(f"{t}_ve", [r, q]) for t, (r, q, _) in LN.items()}
        rs = {t: sb(f"{t}_rs", [r, q]) for t, (r, q, _) in LN.items()}
        nXT = sb("nXT", [P, C, SKV])
        lmx = sb("lmx", [P, QT])
        lnm = sb("lnm", [P, QT])
        lp = sb("lp", [P, QT, SKV])
        lsum = sb("lsum", [P, QT])
        lrec = sb("lrec", [P, QT])
        lpT = sb("lpT", [SKV, T])
        xf = sb("xf", [SKV, FC])
        g5 = sb("g5", [FC + 1, T])
        smx = sb("smx", [P, QT])
        snm = sb("snm", [P, QT])
        ssum = sb("ssum", [P, QT])
        srec = sb("srec", [P, QT])

        ring = [st.enter_context(nc.psum_tensor(f"ring{i}", [P, 2, 512], F32)) for i in range(2)]
        maxT_ps = st.enter_context(nc.psum_tensor("maxT_ps", [P, 512], F32))
        od = st.enter_context(nc.psum_tensor("od", [P, 2, T], F32))
        mring = [st.enter_context(nc.psum_tensor(f"mring{i}", [P, 512], F32)) for i in range(2)]

        s_w = {n: sem(f"w_loaded_{n}") for n in W_ORDER}
        s_small = sem("small_loaded")
        N_SMALL = 5 + len(ROWS) // QT
        s_whi = sem("weights_hi")
        s_wlo = sem("weights_lo")
        s_cz = sem("const_zeroed")
        s_cset = sem("const_set")
        s_vset = sem("const_vector_set")
        s_bcmm = sem("rows_broadcast_mm")
        s_bc = sem("rows_broadcast")
        x_in = sig("x_in", 16)
        c_in = sig("ctx_in", 16)
        cl_in = sig("ctx_l_in", 16)
        stored = sig("stored", 16)
        S = {}
        for t in ("sa", "ca", "mlp"):
            for k, per in (("ss", QT), ("ms", 1), ("rstd", 1), ("xn", QT), ("T", 1), ("hi", C), ("lo", C)):
                S[t, k] = sig(f"{t}_{k}", per)
        for t, fills in (("sa", 8), ("ca", 4)):
            for k, per in (("qkmm", 1), ("qkhi", 2), ("qklo", 2), ("vmm", 1), ("vz", 2), ("pqmm", 2), ("pkmm", 2 if t == "sa" else 1),
                           ("pq", 2), ("pk", 2 if t == "sa" else 1), ("S", fills), ("mx", 8), ("nm", 8),
                           ("maxT", 2), ("negT", 2), ("E", fills), ("exp", fills), ("pv", 4 if t == "sa" else 2), ("rD", 2),
                           ("at", 2), ("athi", 2), ("atlo", 2), ("wo", 1), ("res", 1)):
                S[t, k] = sig(f"{t}_{k}", per)
        for k, per in (("cTmm", 1), ("cThi", 1), ("cTlo", 1)):
            S[k] = sig(k, per)
        for k, per in (("gu", M), ("tanh", M), ("ga", M), ("hid", M), ("hidhi", M), ("hidlo", M), ("dn", 1), ("h3", 1),
                       ("nFTmm", 1), ("nFT", 1), ("nXTmm", 1), ("nXT", 1), ("scmm", 1), ("lmx", 1), ("lnm", 1),
                       ("lp", QT), ("xf", 1), ("lrec", 1), ("lpn", QT), ("pTmm", 1), ("lpT", 1), ("h4", 1), ("g5", 1),
                       ("f2", 1), ("cross", 1), ("nCTmm", 1), ("nCT", 1), ("s2", 1), ("smx", 1), ("snm", 1),
                       ("sp2", QT), ("srec", 1), ("p2Tmm", 1), ("p2T", 1), ("pv2", 1), ("t1", QT), ("t2", QT),
                       ("t3", QT), ("o", QT)):
            S[k] = sig(k, per)
        for t, (_, q, _) in LN.items():
            for k, per in (("st", q), ("mv", q), ("ve", 1), ("rs", 1), ("cen", q), ("scl", q), ("nrm", q)):
                S[t, k] = sig(f"{t}_{k}", per)

        STAGE_COL = [512 * k for k in range(8)] + [0, 2048, 0]
        STAGE_AFTER = [0] * 8 + [4, 8, 9]

        def stage_of(k):
            cols = 512 if k < len(ATTN_W) else 2048
            return probs[:].rearrange("p g i h t -> p (g i h t)")[:, STAGE_COL[k]:STAGE_COL[k] + cols]

        def freed(name):
            if isinstance(name, str):
                if name.startswith("gu"):
                    return S["hid"], int(name[2:]) + 1
                return {"mT": (S["mlp", "lo"], C), "dn": (S["h3"], 1), "nFT": (S["nFT"], 1), "nXT": (S["nXT"], 1),
                        "sc": (S["xf"], 1), "pT": (S["lpT"], 1), "h4": (S["g5"], 1), "f2": (S["cross"], 1),
                        "nCT": (S["nCT"], 1), "s2": (S["sp2"], QT), "p2T": (S["p2T"], 1), "pv2": (S["t1"], QT)}[name]
            tag, kind, k = (*name, 0)[:3]
            return {"T": lambda: (S[tag, "lo"], C), "qk": lambda: (S[tag, "qklo"], 2), "v": lambda: (S[tag, "vz"], 2),
                    "pq": lambda: (S[tag, "pq"], k + 1), "pk": lambda: (S[tag, "pk"], k + 1),
                    "S": lambda: (S[tag, "mx"], (k + 1) * (1 if tag == "sa" else 2)),
                    "E": lambda: (S[tag, "exp"], k + 1), "wo": lambda: (S[tag, "res"], 1),
                    "cT": lambda: (S["cTlo"], 1)}[kind]()

        def ring_tile(name):
            return ring[A_FILLS.index(name) % 2]

        def mring_tile(name):
            return mring[M_FILLS.index(name) % 2]

        SPLIT = {t: (hT_m if t == "mlp" else hT_a) for t in NORM_AT}
        XN = {"sa": xn_a, "ca": xn_a, "mlp": xn_m}
        NORM_SRC = {"sa": x_sb, "ca": h1, "mlp": h2}

        def wait_norm_source(eng, tag, n):
            if tag == "sa":
                eng.wait_ge(x_in.sem, x_in.at(n, 16))
            else:
                eng.wait_ge(S[{"ca": "sa", "mlp": "ca"}[tag], "res"].sem, S[{"ca": "sa", "mlp": "ca"}[tag], "res"].at(n, 1))

        def norm_tile(tag):
            return mring_tile("mT") if tag == "mlp" else ring_tile((tag, "T"))[:, 0, :]

        def pair_head(k, tag):
            return (k // 4, k % 4, 1) if tag == "sa" else (k // 2, 2 * (k % 2), 2)

        def shifted_at(k, tag):
            tiles = QT if tag == "sa" else 1
            return k // (2 * tiles), (k // 2) % tiles, 2 * (k % 2), k // 2

        def granule(g, tag):
            return probs[:, g % GRANULES]

        def run(eng, todo):
            def one(it, tracks):
                for step in ITERATION:
                    f = todo.get(step[0])
                    if f and track(step) in tracks:
                        f(it + track(step), *step[1:])

            one(-1, (1,))
            one(0, (0, 1))
            one(1, (-1, 0, 1))
            with eng.Fori(2, B - 1) as it:
                one(it, (-1, 0, 1))
            one(B - 1, (-1, 0))
            one(B, (-1,))

        block = st.enter_context(nc.Block())

        @block.sync
        def _(sp):
            x_v = x.rearrange("b (q p) d -> b p q d", p=P)
            o_v = out.rearrange("b (q p) d -> b p q d", p=P)
            sp.dma_start(x_sb[:], x_v[0]).then_inc(x_in.sem, 16)
            sp.dma_start(normw[:].rearrange("p n c -> p (n c)"), norm_w).then_inc(s_small, 16)
            for k in range(0, len(ROWS), QT):
                sp.dma_start(buf[k // QT][0:1, :, :], vecs[k:k + QT, :].rearrange("(o n) d -> o n d", o=1)).then_inc(s_small, 16)
            sp.dma_start(fc1t_sb[:], fc1t.rearrange("(c p) h -> p c h", p=P)).then_inc(s_small, 16)
            sp.dma_start(fc1b_sb[:], fc1b.rearrange("(h o) -> h o", o=1)).then_inc(s_small, 16)
            sp.dma_start(fc2_sb[0:FC, :], fc2t).then_inc(s_small, 16)
            sp.dma_start(fc2_sb[FC:FC + 1, :], fc2b.rearrange("(o d) -> o d", o=1)).then_inc(s_small, 16)
            for k, n in enumerate(W_ORDER):
                if STAGE_AFTER[k]:
                    sp.wait_ge(s_wlo, STAGE_AFTER[k])
                sp.dma_start(stage_of(k).rearrange("p (c n) -> p c n", n=w[n].shape[1]),
                             w[n].rearrange("(c p) n -> p c n", p=P)).then_inc(s_w[n], 16)
            sp.dma_start(ctx_sb[:], ctx[0]).then_inc(c_in.sem, 16)

            def load_x(n, *_):
                if not_first(n):
                    sp.wait_ge(S["sa", "res"].sem, S["sa", "res"].at(n - 1, 1))
                sp.dma_start(x_sb[:], x_v[n]).then_inc(x_in.sem, 16)
                if not_first(n):
                    sp.wait_ge(S["cTmm"].sem, S["cTmm"].at(n - 1, 1))
                sp.dma_start(ctx_sb[:], ctx[n]).then_inc(c_in.sem, 16)

            def load_ctx_l(n):
                if not_first(n):
                    sp.wait_ge(S["nXTmm"].sem, S["nXTmm"].at(n - 1, 1))
                sp.dma_start(ctx_l[:, 0, :], ctx[n]).then_inc(cl_in.sem, 16)

            def store(n):
                sp.wait_ge(S["o"].sem, S["o"].at(n, QT))
                sp.dma_start(o_v[n], o_sb[:]).then_inc(stored.sem, 16)

            load_x(1)
            load_ctx_l(0)
            load_x(2)
            load_ctx_l(1)
            store(0)
            with sp.Fori(2, B - 1) as it:
                load_x(it + 1)
                load_ctx_l(it)
                store(it - 1)
            load_ctx_l(B - 1)
            store(B - 2)
            store(B - 1)
            sp.wait_ge(stored.sem, stored.at(B - 1, 16))

        @block.gpsimd
        def _(pool):
            nc.gpsimd.memset(ident[:], 0.0).then_inc(s_cz, 1)
            nc.gpsimd.memset(sel[:].bitcast(F32), 0.0).then_inc(s_cz, 1)
            nc.gpsimd.memset(maxsel[:].bitcast(F32), 0.0).then_inc(s_cz, 1)
            pool.wait_ge(s_cz, 3)
            nc.gpsimd.affine_select(out=ident[:], in_=ident[:], compare_op=ALU.not_equal, fill=1.0, base=0,
                                    pattern=[[-1, P]], channel_multiplier=1).then_inc(s_cset, 1)
            for kind, r0, step in ((0, 0, 2), (1, 1, 2), (2, 0, 1), (3, 2, 1)):
                for i in range(PAIRS):
                    v = sel[:, kind, i, :].rearrange("p (h r d) -> p h r d", h=2, r=4)[:, :, r0:r0 + step + 1:step, :]
                    nc.gpsimd.affine_select(out=v, in_=v.bitcast(F32), compare_op=ALU.not_equal, fill=1.0, base=-32 * i,
                                            pattern=[[-16, 2], [0, 2], [-1, 16]], channel_multiplier=1).then_inc(s_cset, 1)
            for part, base in enumerate((0, 8, 64, 72)):
                if part:
                    pool.wait_ge(s_cset, 1 + 4 * PAIRS + part)
                nc.gpsimd.affine_select(out=maxsel[:], in_=maxsel[:].bitcast(F32), compare_op=ALU.not_equal, fill=1.0,
                                        base=-base, pattern=[[-1, 8], [0, 2]], channel_multiplier=1).then_inc(s_cset, 1)

            def norm(n, tag):
                pool.wait_ge(S[tag, "ms"].sem, S[tag, "ms"].at(n, 1))
                nc.gpsimd.tensor_tensor(rstd[tag][:], ms[tag][:], half_neg[:], ALU.pow).then_inc(S[tag, "rstd"].sem, 1)

            def normalised(n, tag, c):
                pool.wait_ge(S[tag, "athi"].sem, S[tag, "athi"].at(n, c + 1))
                nc.gpsimd.tensor_tensor(atT[1][:, c, :], at[:, c, :], atT[0][:, c, :].bitcast(F32), ALU.subtract).then_inc(S[tag, "atlo"].sem, 1)

            def gu(n, m):
                pool.wait_ge(S["hidhi"].sem, S["hidhi"].at(n, m + 1))
                nc.gpsimd.tensor_tensor(hidT[1][:, m, :], hid[:, m % 2, :], hidT[0][:, m, :].bitcast(F32), ALU.subtract).then_inc(S["hidlo"].sem, 1)

            def lnstat(n, tag):
                r, tiles, _ = LN[tag]
                pool.wait_ge(S[tag, "ve"].sem, S[tag, "ve"].at(n, 1))
                nc.gpsimd.tensor_tensor(rs[tag][:], ve[tag][:], half_neg[0:r, 0:tiles], ALU.pow).then_inc(S[tag, "rs"].sem, 1)

            def lncen(n, tag):
                r, tiles, at_row = LN[tag]
                for q in range(tiles):
                    pool.wait_ge(S[tag, "cen"].sem, S[tag, "cen"].at(n, q + 1))
                    nc.gpsimd.tensor_tensor(NRM[tag][:, q, :], NRM[tag][:, q, :], bc[0:r, at_row, :], ALU.mult).then_inc(S[tag, "scl"].sem, 1)
                for q in range(tiles):
                    pool.wait_ge(S[tag, "scl"].sem, S[tag, "scl"].at(n, q + 1))
                    nc.gpsimd.tensor_tensor(NRM[tag][:, q, :], NRM[tag][:, q, :], bc[0:r, at_row + 1, :], ALU.add).then_inc(S[tag, "nrm"].sem, 1)

            def out_(n):
                for q in range(QT):
                    pool.wait_ge(S["t1"].sem, S["t1"].at(n, q + 1))
                    nc.gpsimd.tensor_tensor(t1[:, q, :], t1[:, q, :], cross[:, q, :], ALU.add).then_inc(S["t2"].sem, 1)
                for q in range(QT):
                    pool.wait_ge(S["t2"].sem, S["t2"].at(n, q + 1))
                    nc.gpsimd.tensor_tensor(t1[:, q, :], t1[:, q, :], bc[:, 7, :], ALU.mult).then_inc(S["t3"].sem, 1)
                if not_first(n):
                    pool.wait_ge(stored.sem, stored.at(n - 1, 16))
                for q in range(QT):
                    pool.wait_ge(S["t3"].sem, S["t3"].at(n, q + 1))
                    nc.gpsimd.tensor_tensor(o_sb[:, q, :], t1[:, q, :], nF[:, q, :], ALU.add).then_inc(S["o"].sem, 1)

            pool.wait_ge(s_bc, 2)
            pool.wait_ge(s_vset, 5)
            run(pool, {"norm": norm, "at": normalised, "gu": gu, "lnstat": lnstat, "lncen": lncen, "out": out_})

        @block.scalar
        def _(act):
            for k, n in enumerate(W_ORDER):
                act.wait_ge(s_w[n], 16)
                nc.scalar.activation(wt[n][0][:].rearrange("p c n -> p (c n)"), stage_of(k), ACT.Copy).then_inc(s_whi, 1)
            act.wait_ge(s_bcmm, 1)
            for b in range(2):
                nc.scalar.activation(bc[:, 4 * b:4 * b + 4, :], ring[b][:].rearrange("p b (r d) -> p (b r) d", d=D), ACT.Copy).then_inc(s_bc, 1)
            act.wait_ge(s_small, 16 * N_SMALL)
            act.wait_ge(s_wlo, len(W_ORDER))

            def norm(n, tag):
                wait_norm_source(act, tag, n)
                for q in range(QT):
                    nc.scalar.activation(XN[tag][:, q, :], NORM_SRC[tag][:, q, :], ACT.Square,
                                         accum_out=ss[tag][:, q:q + 1]).then_inc(S[tag, "ss"].sem, 1)

            def transposed(n, tag):
                act.wait_ge(S[tag, "T"].sem, S[tag, "T"].at(n, 1))
                ps = norm_tile(tag)
                for c in range(C):
                    nc.scalar.activation(SPLIT[tag][0][:, c, :], ps[:, c * T:(c + 1) * T], ACT.Copy,
                                         scale=normw[:, NORM_AT[tag], c:c + 1]).then_inc(S[tag, "hi"].sem, 1)

            def ctx_transposed(n, tag):
                act.wait_ge(S["cTmm"].sem, S["cTmm"].at(n, 1))
                ps = ring_tile(("ca", "cT"))[:, 0, 0:C * SKV].rearrange("p (c t) -> p c t", c=C)
                nc.scalar.activation(cT[0][:, :, 0:SKV], ps, ACT.Copy).then_inc(S["cThi"].sem, 1)

            def qk(n, tag):
                act.wait_ge(S[tag, "qkmm"].sem, S[tag, "qkmm"].at(n, 1))
                ps = ring_tile((tag, "qk"))
                kw = T if tag == "sa" else SKV2
                nc.scalar.activation(qT[0][:], ps[:, 0, :].rearrange("p (c t) -> p c t", c=C), ACT.Copy).then_inc(S[tag, "qkhi"].sem, 1)
                nc.scalar.activation(kT[0][:, :, 0:kw], ps[:, 1, 0:C * kw].rearrange("p (c t) -> p c t", c=C), ACT.Copy).then_inc(S[tag, "qkhi"].sem, 1)

            def v(n, tag):
                act.wait_ge(S[tag, "vmm"].sem, S[tag, "vmm"].at(n, 1))
                rows_, tiles = (P, QT) if tag == "sa" else (SKV, 1)
                ps = ring_tile((tag, "v"))[0:rows_, 0, 0:tiles * D].rearrange("p (k s h d) -> p k s h d", k=tiles, h=2, d=HD)
                vv = vz[0:rows_, 0:tiles].rearrange("p k (s h) e -> p k s h e", h=2)
                for half in range(2):
                    nc.scalar.activation(vv[:, :, :, half, half * HD:(half + 1) * HD], ps[:, :, :, half, :], ACT.Copy).then_inc(S[tag, "vz"].sem, 1)

            def pack(n, tag, c):
                act.wait_ge(S[tag, "pqmm"].sem, S[tag, "pqmm"].at(n, c + 1))
                ps = ring_tile((tag, "pq", c))[:].rearrange("p b (s t) -> p (b s) t", t=T)
                nc.scalar.activation(qpk[:, PAIRS * c:PAIRS * (c + 1), :], ps, ACT.Copy).then_inc(S[tag, "pq"].sem, 1)

            def exps(n, tag, k):
                act.wait_ge(S[tag, "E"].sem, S[tag, "E"].at(n, k + 1))
                c, kt, i0, g = shifted_at(k, tag)
                if k % 2 == 0:
                    if g >= GRANULES:
                        act.wait_ge(S[tag, "pv"].sem, S[tag, "pv"].at(n, g - GRANULES + 1))
                    elif tag == "ca":
                        act.wait_ge(S["sa", "pv"].sem, S["sa", "pv"].at(n, 4 - GRANULES + g + 1))
                    else:
                        if not_first(n):
                            act.wait_ge(S["ca", "pv"].sem, S["ca", "pv"].at(n - 1, 2 - GRANULES + g + 1))
                rows_ = P if tag == "sa" else SKV
                nc.scalar.activation(granule(g, tag)[0:rows_, i0:i0 + 2, :, :].rearrange("p i h t -> p h i t"),
                                     ring_tile((tag, "E", k))[0:rows_].rearrange("p h (i t) -> p h i t", t=T),
                                     ACT.Exp, scale=HEAD_SCALE).then_inc(S[tag, "exp"].sem, 1)

            def normalised(n, tag, c):
                act.wait_ge(S[tag, "at"].sem, S[tag, "at"].at(n, c + 1))
                nc.scalar.activation(atT[0][:, c, :], at[:, c, :], ACT.Copy).then_inc(S[tag, "athi"].sem, 1)

            def gu(n, m):
                act.wait_ge(S["gu"].sem, S["gu"].at(n, m + 1))
                if m >= 2:
                    act.wait_ge(S["hidlo"].sem, S["hidlo"].at(n, m - 1))
                nc.scalar.activation(hid[:, m % 2, :], mring_tile(f"gu{m}")[:, 0:T], ACT.Tanh, scale=0.5).then_inc(S["tanh"].sem, 1)
                act.wait_ge(S["hid"].sem, S["hid"].at(n, m + 1))
                nc.scalar.activation(hidT[0][:, m, :], hid[:, m % 2, :], ACT.Copy).then_inc(S["hidhi"].sem, 1)

            def evacuate(signal, done, fill, dst, rows_, cols):
                def f(n):
                    act.wait_ge(S[signal].sem, S[signal].at(n, 1))
                    nc.scalar.activation(dst, mring_tile(fill)[0:rows_, 0:cols], ACT.Copy).then_inc(S[done].sem, 1)
                return f

            def sc(n):
                act.wait_ge(S["lnm"].sem, S["lnm"].at(n, 1))
                for q in range(QT):
                    nc.scalar.activation(lp[:, q, :], mring_tile("sc")[:, q * SKV:(q + 1) * SKV], ACT.Exp,
                                         bias=lnm[:, q:q + 1], scale=L1_SCALE, accum_out=lsum[:, q:q + 1]).then_inc(S["lp"].sem, 1)
                nc.scalar.activation(xf[:], mring_tile("sc")[0:SKV, QT * SKV:QT * SKV + FC], ACT.Copy).then_inc(S["xf"].sem, 1)

            def h4(n):
                act.wait_ge(S["h4"].sem, S["h4"].at(n, 1))
                nc.scalar.activation(g5[0:FC, :], mring_tile("h4")[0:FC, 0:T], ACT.Gelu, bias=fc1b_sb[:, 0:1]).then_inc(S["g5"].sem, 1)

            def s2(n):
                act.wait_ge(S["snm"].sem, S["snm"].at(n, 1))
                for q in range(QT):
                    nc.scalar.activation(sp2[:, q, :], mring_tile("s2")[:, q * T:(q + 1) * T], ACT.Exp,
                                         bias=snm[:, q:q + 1], scale=L1_SCALE, accum_out=ssum[:, q:q + 1]).then_inc(S["sp2"].sem, 1)

            flat = lambda t: t[:].rearrange("p c t -> p (c t)")
            run(act, {"norm": norm, "T": transposed, "cT": ctx_transposed, "qk": qk, "v": v, "pack": pack, "E": exps, "at": normalised, "gu": gu,
                      "nFT": evacuate("nFTmm", "nFT", "nFT", flat(nFT), P, C * T),
                      "nXT": evacuate("nXTmm", "nXT", "nXT", flat(nXT), P, C * SKV),
                      "sc": sc, "pT": evacuate("pTmm", "lpT", "pT", lpT[:], SKV, T), "h4": h4,
                      "f2": evacuate("f2", "cross", "f2", flat(cross), P, QT * D),
                      "nCT": evacuate("nCTmm", "nCT", "nCT", flat(nCT), P, C * T), "s2": s2,
                      "p2T": evacuate("p2Tmm", "p2T", "p2T", flat(p2T), P, QT * T)})

        @block.vector
        def _(dve):
            nc.vector.memset(ones_row[:], 1.0).then_inc(s_vset, 1)
            nc.vector.memset(half_neg[:], -0.5).then_inc(s_vset, 1)
            nc.vector.memset(vz[:], 0.0).then_inc(s_vset, 1)
            nc.vector.memset(g5[:], 1.0).then_inc(s_vset, 1)
            nc.vector.memset(negT[:].bitcast(F32), 0.0).then_inc(s_vset, 1)
            for p in range(2):
                nc.vector.memset(cT[p][:].bitcast(F32), 0.0).then_inc(s_vset, 1)
            nc.vector.memset(ones_pad[:], 0.0).then_inc(s_vset, 1)
            nc.vector.memset(nm[:], 0.0).then_inc(s_vset, 1)
            dve.wait_ge(s_vset, 9)
            for half in range(2):
                nc.vector.memset(ones_pad[:, half, half * HD:(half + 1) * HD], 1.0).then_inc(s_vset, 1)
            for k, n in enumerate(W_ORDER):
                dve.wait_ge(s_whi, k + 1)
                hi, lo = (t[:].rearrange("p c n -> p (c n)") for t in wt[n])
                nc.vector.tensor_tensor(lo, stage_of(k), hi.bitcast(F32), ALU.subtract).then_inc(s_wlo, 1)

            def norm(n, tag):
                dve.wait_ge(S[tag, "ss"].sem, S[tag, "ss"].at(n, QT))
                nc.vector.tensor_scalar(ms[tag][:], ss[tag][:], 1.0 / D, RMS_EPS, ALU.mult, ALU.add).then_inc(S[tag, "ms"].sem, 1)

            def xn(n, tag):
                dve.wait_ge(S[tag, "rstd"].sem, S[tag, "rstd"].at(n, 1))
                wait_norm_source(dve, tag, n)
                for q in range(QT):
                    nc.vector.tensor_scalar(XN[tag][:, q, :], NORM_SRC[tag][:, q, :], rstd[tag][:, q:q + 1], None, ALU.mult).then_inc(S[tag, "xn"].sem, 1)

            def transposed(n, tag):
                dve.wait_ge(S[tag, "hi"].sem, S[tag, "hi"].at(n, C))
                ps = norm_tile(tag)
                for c in range(C):
                    nc.vector.scalar_tensor_tensor(out=SPLIT[tag][1][:, c, :], in0=ps[:, c * T:(c + 1) * T],
                                                   scalar=normw[:, NORM_AT[tag], c:c + 1], in1=SPLIT[tag][0][:, c, :].bitcast(F32),
                                                   op0=ALU.mult, op1=ALU.subtract).then_inc(S[tag, "lo"].sem, 1)

            def ctx_transposed(n, tag):
                dve.wait_ge(S["cThi"].sem, S["cThi"].at(n, 1))
                ps = ring_tile(("ca", "cT"))[:, 0, 0:C * SKV].rearrange("p (c t) -> p c t", c=C)
                nc.vector.tensor_tensor(cT[1][:, :, 0:SKV], ps, cT[0][:, :, 0:SKV].bitcast(F32), ALU.subtract).then_inc(S["cTlo"].sem, 1)

            def qk(n, tag):
                ps = ring_tile((tag, "qk"))
                kw = T if tag == "sa" else SKV2
                dve.wait_ge(S[tag, "qkhi"].sem, S[tag, "qkhi"].at(n, 1))
                nc.vector.tensor_tensor(qT[1][:], ps[:, 0, :].rearrange("p (c t) -> p c t", c=C), qT[0][:].bitcast(F32), ALU.subtract).then_inc(S[tag, "qklo"].sem, 1)
                dve.wait_ge(S[tag, "qkhi"].sem, S[tag, "qkhi"].at(n, 2))
                nc.vector.tensor_tensor(kT[1][:, :, 0:kw], ps[:, 1, 0:C * kw].rearrange("p (c t) -> p c t", c=C),
                                        kT[0][:, :, 0:kw].bitcast(F32), ALU.subtract).then_inc(S[tag, "qklo"].sem, 1)

            def pack(n, tag, c):
                if tag == "sa":
                    dve.wait_ge(S[tag, "pkmm"].sem, S[tag, "pkmm"].at(n, c + 1))
                    ps = ring_tile((tag, "pk", c))[:].rearrange("p b (s t) -> p (b s) t", t=T)
                    nc.vector.tensor_copy(kpk[:, PAIRS * c:PAIRS * (c + 1), :], ps).then_inc(S[tag, "pk"].sem, 1)
                elif c == 0:
                    dve.wait_ge(S[tag, "pkmm"].sem, S[tag, "pkmm"].at(n, 1))
                    ps = ring_tile((tag, "pk", 0))[:, :, 0:PAIRS * SKV2].rearrange("p b (s t) -> p b s t", t=SKV2)
                    nc.vector.tensor_copy(kpk[:, :, 0:SKV2].rearrange("p (b s) t -> p b s t", b=2), ps).then_inc(S[tag, "pk"].sem, 1)

            def maxima(n, tag, k):
                dve.wait_ge(S[tag, "S"].sem, S[tag, "S"].at(n, k + 1))
                c, i, pairs = pair_head(k, tag)
                ps = ring_tile((tag, "S", k))
                if tag == "sa":
                    nc.vector.tensor_reduce(mx[:, c, :, 2 * i:2 * i + 2].rearrange("p q h -> p h q"),
                                            ps[:].rearrange("p h (q t) -> p h q t", t=T), AX_X, ALU.max).then_inc(S[tag, "mx"].sem, 1)
                else:
                    for half in range(2):
                        v = ps[:, half, 0:2 * QT * SKV2].rearrange("p (i q t) -> p i q t", i=2, t=SKV2)[:, :, :, 0:SKV]
                        nc.vector.tensor_reduce(mx[:, c, :, 2 * i + half:2 * i + half + 3:2].rearrange("p q i -> p i q"),
                                                v, AX_X, ALU.max).then_inc(S[tag, "mx"].sem, 1)

            def maxsplit(n, tag, c):
                dve.wait_ge(S[tag, "mx"].sem, S[tag, "mx"].at(n, 4 * (c + 1)))
                for at0 in (0, 64):
                    nc.vector.tensor_scalar(nm[:, c, :, at0:at0 + 8].bitcast(F32R), mx[:, c, :, :], -1.0, None, ALU.mult).then_inc(S[tag, "nm"].sem, 1)
                for k, at0 in enumerate((0, 64)):
                    dve.wait_ge(S[tag, "nm"].sem, S[tag, "nm"].at(n, 4 * c + k + 1))
                    nc.vector.scalar_tensor_tensor(out=nm[:, c, :, at0 + 8:at0 + 16], in0=mx[:, c, :, :], scalar=-1.0, in1=nm[:, c, :, at0:at0 + 8],
                                                   op0=ALU.mult, op1=ALU.subtract).then_inc(S[tag, "nm"].sem, 1)

            def maxT(n, tag, c):
                dve.wait_ge(S[tag, "maxT"].sem, S[tag, "maxT"].at(n, c + 1))
                nc.vector.tensor_copy(negT[0:80, c, :], maxT_ps[0:80, 0:T]).then_inc(S[tag, "negT"].sem, 1)

            def normalise(n, tag, c):
                dve.wait_ge(S[tag, "pv"].sem, S[tag, "pv"].at(n, (QT if tag == "sa" else 1) * (c + 1)))
                nc.vector.reciprocal(rD[:], od[:, 1, :]).then_inc(S[tag, "rD"].sem, 1)
                dve.wait_ge(S[tag, "rD"].sem, S[tag, "rD"].at(n, c + 1))
                nc.vector.tensor_tensor(at[:, c, :], od[:, 0, :], rD[:], ALU.mult).then_inc(S[tag, "at"].sem, 1)

            def wo(n, tag):
                dve.wait_ge(S[tag, "wo"].sem, S[tag, "wo"].at(n, 1))
                src, dst = (x_sb, h1) if tag == "sa" else (h1, h2)
                ps = ring_tile((tag, "wo"))[:, 0, :].rearrange("p (q d) -> p q d", q=QT)
                nc.vector.tensor_tensor(dst[:], src[:], ps, ALU.add).then_inc(S[tag, "res"].sem, 1)

            def gu(n, m):
                ps = mring_tile(f"gu{m}")
                dve.wait_ge(S["tanh"].sem, S["tanh"].at(n, m + 1))
                nc.vector.scalar_tensor_tensor(out=hid[:, m % 2, :], in0=hid[:, m % 2, :], scalar=1.0, in1=ps[:, 0:T], op0=ALU.add, op1=ALU.mult).then_inc(S["ga"].sem, 1)
                dve.wait_ge(S["ga"].sem, S["ga"].at(n, m + 1))
                nc.vector.scalar_tensor_tensor(out=hid[:, m % 2, :], in0=hid[:, m % 2, :], scalar=0.5, in1=ps[:, T:2 * T], op0=ALU.mult, op1=ALU.mult).then_inc(S["hid"].sem, 1)

            def dn(n):
                dve.wait_ge(S["dn"].sem, S["dn"].at(n, 1))
                nc.vector.tensor_tensor(h3[:], h2[:], mring_tile("dn")[:].rearrange("p (q d) -> p q d", q=QT), ALU.add).then_inc(S["h3"].sem, 1)

            LN_SRC = {"nf": h3, "nx": ctx_l, "nc": cross}

            def lnstat(n, tag):
                r, tiles, _ = LN[tag]
                if tag == "nx":
                    dve.wait_ge(cl_in.sem, cl_in.at(n, 16))
                else:
                    dve.wait_ge(S[{"nf": "h3", "nc": "cross"}[tag]].sem, S[{"nf": "h3", "nc": "cross"}[tag]].at(n, 1))
                src = [LN_SRC[tag][:, q, :] for q in range(tiles)]
                for q in range(tiles):
                    nc.vector.bn_stats(stats[tag][:, q, :], src[q]).then_inc(S[tag, "st"].sem, 1)
                dve.wait_ge(S[tag, "st"].sem, S[tag, "st"].at(n, tiles))
                nc.vector.memset(ve[tag][:], LN_EPS)
                for q in range(tiles):
                    nc.vector.bn_aggr(mv[tag][:, q, :], stats[tag][:, q, :]).then_inc(S[tag, "mv"].sem, 1)
                dve.wait_ge(S[tag, "mv"].sem, S[tag, "mv"].at(n, tiles))
                nc.vector.tensor_tensor(ve[tag][:], ve[tag][:], mv[tag][:, :, 1], ALU.add).then_inc(S[tag, "ve"].sem, 1)

            def lncen(n, tag):
                src, tiles = LN_SRC[tag], LN[tag][1]
                dve.wait_ge(S[tag, "rs"].sem, S[tag, "rs"].at(n, 1))
                for q in range(tiles):
                    nc.vector.tensor_scalar(NRM[tag][:, q, :], src[:, q, :], mv[tag][:, q, 0:1], rs[tag][:, q:q + 1],
                                            ALU.subtract, ALU.mult).then_inc(S[tag, "cen"].sem, 1)

            def sc(n):
                dve.wait_ge(S["scmm"].sem, S["scmm"].at(n, 1))
                nc.vector.tensor_reduce(lmx[:], mring_tile("sc")[:, 0:QT * SKV].rearrange("p (q t) -> p q t", q=QT), AX_X, ALU.max).then_inc(S["lmx"].sem, 1)
                dve.wait_ge(S["lmx"].sem, S["lmx"].at(n, 1))
                nc.vector.tensor_scalar(lnm[:], lmx[:], -L1_SCALE, None, ALU.mult).then_inc(S["lnm"].sem, 1)
                dve.wait_ge(S["lp"].sem, S["lp"].at(n, QT))
                nc.vector.reciprocal(lrec[:], lsum[:]).then_inc(S["lrec"].sem, 1)
                dve.wait_ge(S["lrec"].sem, S["lrec"].at(n, 1))
                for q in range(QT):
                    nc.vector.tensor_scalar(lp[:, q, :], lp[:, q, :], lrec[:, q:q + 1], None, ALU.mult).then_inc(S["lpn"].sem, 1)

            def s2(n):
                dve.wait_ge(S["s2"].sem, S["s2"].at(n, 1))
                nc.vector.tensor_reduce(smx[:], mring_tile("s2")[:].rearrange("p (q t) -> p q t", q=QT), AX_X, ALU.max).then_inc(S["smx"].sem, 1)
                dve.wait_ge(S["smx"].sem, S["smx"].at(n, 1))
                nc.vector.tensor_scalar(snm[:], smx[:], -L1_SCALE, None, ALU.mult).then_inc(S["snm"].sem, 1)
                dve.wait_ge(S["sp2"].sem, S["sp2"].at(n, QT))
                nc.vector.reciprocal(srec[:], ssum[:]).then_inc(S["srec"].sem, 1)

            def pv2(n):
                dve.wait_ge(S["pv2"].sem, S["pv2"].at(n, 1))
                dve.wait_ge(S["srec"].sem, S["srec"].at(n, 1))
                for q in range(QT):
                    nc.vector.scalar_tensor_tensor(out=t1[:, q, :], in0=mring_tile("pv2")[:, q * D:(q + 1) * D], scalar=srec[:, q:q + 1],
                                                   in1=bc[:, 6, :], op0=ALU.mult, op1=ALU.mult).then_inc(S["t1"].sem, 1)

            dve.wait_ge(s_small, 16 * N_SMALL)
            dve.wait_ge(s_bc, 2)
            run(dve, {"norm": norm, "xn": xn, "T": transposed, "cT": ctx_transposed, "qk": qk, "pack": pack, "S": maxima, "maxsplit": maxsplit,
                      "maxT": maxT, "at": normalise, "wo": wo, "gu": gu, "dn": dn, "lnstat": lnstat, "lncen": lncen, "sc": sc, "s2": s2, "pv2": pv2})

        @block.tensor
        def _(pe):
            mm = nc.tensor.matmul
            pe.wait_ge(s_small, 16 * N_SMALL)
            pe.wait_ge(s_vset, 11)
            for k in range(len(ROWS)):
                last = mm(ring[k // 4][:, (k // 2) % 2, (k % 2) * D:(k % 2 + 1) * D], ones_row[:], row_of(k), start=True, stop=True)
            last.then_inc(s_bcmm, 1)
            pe.wait_ge(s_bc, 2)
            pe.wait_ge(s_cset, 1 + 4 * PAIRS + 4)
            pe.wait_ge(s_wlo, len(W_ORDER))

            def exists(n):
                return not isinstance(n, int) or 0 <= n < B

            def fill(n, name):
                k = A_FILLS.index(name)
                it, last = n - A_AHEAD[k], k - 2
                while last >= k - len(A_FILLS) and not exists(it + A_AHEAD[last] - int(last < 0)):
                    last -= 2
                if last >= k - len(A_FILLS):
                    signal, j = freed(A_FILLS[last])
                    pe.wait_ge(signal.sem, signal.at(it + A_AHEAD[last] - int(last < 0), j))
                return ring[k % 2]

            def mfill(n, name):
                k = M_FILLS.index(name)
                if k >= 2 or not_first(n):
                    signal, j = freed(M_FILLS[k - 2])
                    pe.wait_ge(signal.sem, signal.at(n - int(k < 2), j))
                return mring[k % 2]

            def product(outs, left, right, chunks):
                total = len(PARTS) * chunks
                for k in range(total):
                    a, b = PARTS[k // chunks]
                    last = mm(outs, left(a, k % chunks), right(b, k % chunks), start=(k == 0), stop=(k == total - 1))
                return last

            def transposed(n, tag):
                pe.wait_ge(S[tag, "xn"].sem, S[tag, "xn"].at(n, QT))
                ps = mfill(n, "mT") if tag == "mlp" else fill(n, (tag, "T"))[:, 0, :]
                for c in range(C):
                    for q in range(QT):
                        last = nc.tensor.transpose(ps[:, c * T + q * P:c * T + (q + 1) * P], XN[tag][:, q, c * P:(c + 1) * P], ident[:])
                last.then_inc(S[tag, "T"].sem, 1)

            def ctx_transposed(n, tag):
                pe.wait_ge(c_in.sem, c_in.at(n, 16))
                ps = fill(n, ("ca", "cT"))
                for c in range(C):
                    last = nc.tensor.transpose(ps[:, 0, c * SKV:(c + 1) * SKV], ctx_sb[:, c * P:(c + 1) * P], ident[0:SKV, 0:SKV])
                last.then_inc(S["cTmm"].sem, 1)

            def qk(n, tag):
                pe.wait_ge(S[tag, "lo"].sem, S[tag, "lo"].at(n, C))
                if tag == "ca":
                    pe.wait_ge(S["cTlo"].sem, S["cTlo"].at(n, 1))
                ps = fill(n, (tag, "qk"))
                wq, wk = wt[f"{tag}_wq"], wt[f"{tag}_wk"]
                src, kw = (hT_a, T) if tag == "sa" else (cT, SKV2)
                for m in range(C):
                    product(ps[:, 0, m * T:(m + 1) * T], lambda a, kc: wq[a][:, kc, m * P:(m + 1) * P], lambda b, kc: hT_a[b][:, kc, :], C)
                for m in range(C):
                    last = product(ps[:, 1, m * kw:(m + 1) * kw], lambda a, kc: wk[a][:, kc, m * P:(m + 1) * P], lambda b, kc: src[b][:, kc, :], C)
                last.then_inc(S[tag, "qkmm"].sem, 1)

            def v(n, tag):
                ps = fill(n, (tag, "v"))
                wv = wt[f"{tag}_wv"]
                for q in range(QT if tag == "sa" else 1):
                    if tag == "sa":
                        last = product(ps[:, 0, q * D:(q + 1) * D], lambda a, kc: hT_a[a][:, kc, q * P:(q + 1) * P], lambda b, kc: wv[b][:, kc, :], C)
                    else:
                        last = product(ps[0:SKV, 0, 0:D], lambda a, kc: cT[a][:, kc, 0:SKV], lambda b, kc: wv[b][:, kc, :], C)
                last.then_inc(S[tag, "vmm"].sem, 1)

            def pack(n, tag, c):
                pe.wait_ge(S[tag, "qklo"].sem, S[tag, "qklo"].at(n, 2))
                ps = fill(n, (tag, "pq", c))
                for i in range(PAIRS):
                    for part in range(2):
                        last = mm(ps[:, i // 2, (i % 2) * T:(i % 2 + 1) * T], sel[:, part, i, :], qT[part][:, c, :], start=(part == 0), stop=(part == 1))
                last.then_inc(S[tag, "pqmm"].sem, 1)
                if tag == "sa":
                    ps = fill(n, (tag, "pk", c))
                    for i in range(PAIRS):
                        for part in range(2):
                            last = mm(ps[:, i // 2, (i % 2) * T:(i % 2 + 1) * T], sel[:, 2 + part, i, :], kT[part][:, c, :], start=(part == 0), stop=(part == 1))
                    last.then_inc(S[tag, "pkmm"].sem, 1)
                elif c == 0:
                    ps = fill(n, (tag, "pk", 0))
                    for cc in range(C):
                        for i in range(PAIRS):
                            for part in range(2):
                                last = mm(ps[:, cc, i * SKV2:(i + 1) * SKV2], sel[:, 2 + part, i, :], kT[part][:, cc, 0:SKV2], start=(part == 0), stop=(part == 1))
                    last.then_inc(S[tag, "pkmm"].sem, 1)

            def scores(n, tag, k):
                c, i0, pairs = pair_head(k, tag)
                ps = fill(n, (tag, "S", k))
                kw = T if tag == "sa" else SKV2
                for i in range(pairs):
                    for q in range(QT):
                        for half in range(2):
                            r = slice(64 * half, 64 * half + 64)
                            col = (i * QT + q) * kw
                            last = mm(ps[:, half, col:col + kw], qpk[r, PAIRS * c + i0 + i, q * P:(q + 1) * P], kpk[r, PAIRS * c + i0 + i, 0:kw], start=True, stop=True)
                last.then_inc(S[tag, "S"].sem, 1)

            def maxT(n, tag, c):
                pe.wait_ge(S[tag, "nm"].sem, S[tag, "nm"].at(n, 4 * (c + 1)))
                if c:
                    pe.wait_ge(S[tag, "negT"].sem, S[tag, "negT"].at(n, 1))
                elif tag == "sa":
                    if not_first(n):
                        pe.wait_ge(S["ca", "negT"].sem, S["ca", "negT"].at(n - 1, 2))
                else:
                    pe.wait_ge(S["sa", "negT"].sem, S["sa", "negT"].at(n, 2))
                for q in range(QT):
                    last = nc.tensor.transpose(maxT_ps[0:80, q * P:(q + 1) * P], nm[:, c, q, :], ident[:])
                last.then_inc(S[tag, "maxT"].sem, 1)

            def shifted(n, tag, k):
                c, kt, i0, g = shifted_at(k, tag)
                pe.wait_ge(S[tag, "negT"].sem, S[tag, "negT"].at(n, c + 1))
                ps = fill(n, (tag, "E", k))
                rows_ = P if tag == "sa" else SKV
                for u in range(2):
                    i = i0 + u
                    for half in range(2):
                        r = slice(64 * half, 64 * half + 64)
                        mm(ps[0:rows_, half, u * T:(u + 1) * T], kpk[r, PAIRS * c + i, kt * P:kt * P + rows_], qpk[r, PAIRS * c + i, :], start=True, stop=False)
                        last = mm(ps[0:rows_, half, u * T:(u + 1) * T], maxsel[r, 2 * i + half, 0:1].to_broadcast([64, rows_]), negT[r, c, :], start=False, stop=True)
                last.then_inc(S[tag, "E"].sem, 1)

            def pv(n, tag, g):
                rows_, tiles = (P, QT) if tag == "sa" else (SKV, 1)
                c, kt = g // tiles, g % tiles
                pe.wait_ge(S[tag, "exp"].sem, S[tag, "exp"].at(n, 2 * (g + 1)))
                if g == 0:
                    pe.wait_ge(S[tag, "vz"].sem, S[tag, "vz"].at(n, 2))
                if kt == 0:
                    if c:
                        pe.wait_ge(S[tag, "at"].sem, S[tag, "at"].at(n, 1))
                    elif tag == "sa":
                        if not_first(n):
                            pe.wait_ge(S["ca", "at"].sem, S["ca", "at"].at(n - 1, 2))
                    else:
                        pe.wait_ge(S["sa", "at"].sem, S["sa", "at"].at(n, 2))
                for half in range(2):
                    for what in range(2):
                        first = kt == 0 and half == 0 and what == 0
                        final = kt == tiles - 1 and half == 1
                        for i in range(PAIRS):
                            lhs = ones_pad[0:rows_, half, :] if what else vz[0:rows_, kt, 8 * c + 2 * i + half, :]
                            last = mm(od[32 * i:32 * i + 32, what, :], lhs, granule(g, tag)[0:rows_, i, half, :],
                                      start=first, stop=final, tile_position=(0, 32 * i), skip_group_check=True)
                last.then_inc(S[tag, "pv"].sem, 1)

            def wo(n, tag):
                pe.wait_ge(S[tag, "athi"].sem, S[tag, "athi"].at(n, 2))
                pe.wait_ge(S[tag, "atlo"].sem, S[tag, "atlo"].at(n, 2))
                ps = fill(n, (tag, "wo"))
                for q in range(QT):
                    last = product(ps[:, 0, q * D:(q + 1) * D], lambda a, kc: atT[a][:, kc, q * P:(q + 1) * P], lambda b, kc: wt[f"{tag}_wo"][b][:, kc, :], C)
                last.then_inc(S[tag, "wo"].sem, 1)

            def gu(n, m):
                if m == 0:
                    pe.wait_ge(S["mlp", "lo"].sem, S["mlp", "lo"].at(n, C))
                ps = mfill(n, f"gu{m}")
                for k, name in enumerate(("gate", "up")):
                    last = product(ps[:, k * T:(k + 1) * T], lambda a, kc: wt[name][a][:, kc, m * P:(m + 1) * P], lambda b, kc: hT_m[b][:, kc, :], C)
                last.then_inc(S["gu"].sem, 1)

            def dn(n):
                pe.wait_ge(S["hidlo"].sem, S["hidlo"].at(n, M))
                ps = mfill(n, "dn")
                for q in range(QT):
                    last = product(ps[:, q * D:(q + 1) * D], lambda a, kc: hidT[a][:, kc, q * P:(q + 1) * P], lambda b, kc: wt["down"][b][:, kc, :], M)
                last.then_inc(S["dn"].sem, 1)

            def transposes(n, name, signal, src, tiles, rows_, cols):
                ps = mfill(n, name)
                for c in range(cols):
                    for q in range(tiles):
                        at0 = (c * tiles + q) * rows_
                        last = nc.tensor.transpose(ps[:, at0:at0 + rows_], src[:, q, c * P:(c + 1) * P], ident[0:rows_, 0:rows_])
                last.then_inc(S[signal].sem, 1)

            def t_nF(n):
                pe.wait_ge(S["nf", "nrm"].sem, S["nf", "nrm"].at(n, QT))
                transposes(n, "nFT", "nFTmm", nF, QT, P, C)

            def t_nX(n):
                pe.wait_ge(S["nx", "nrm"].sem, S["nx", "nrm"].at(n, 1))
                transposes(n, "nXT", "nXTmm", ctx_l, 1, SKV, C)

            def sc(n):
                pe.wait_ge(S["nFT"].sem, S["nFT"].at(n, 1))
                pe.wait_ge(S["nXT"].sem, S["nXT"].at(n, 1))
                ps = mfill(n, "sc")
                for q in range(QT):
                    for c in range(C):
                        mm(ps[:, q * SKV:(q + 1) * SKV], nFT[:, c, q * P:(q + 1) * P], nXT[:, c, :], start=(c == 0), stop=(c == C - 1))
                for c in range(C):
                    last = mm(ps[0:SKV, QT * SKV:QT * SKV + FC], nXT[:, c, :], fc1t_sb[:, c, :], start=(c == 0), stop=(c == C - 1))
                last.then_inc(S["scmm"].sem, 1)

            def pT(n):
                pe.wait_ge(S["lpn"].sem, S["lpn"].at(n, QT))
                ps = mfill(n, "pT")
                for q in range(QT):
                    last = nc.tensor.transpose(ps[0:SKV, q * P:(q + 1) * P], lp[:, q, :], ident[:])
                last.then_inc(S["pTmm"].sem, 1)

            def h4(n):
                pe.wait_ge(S["lpT"].sem, S["lpT"].at(n, 1))
                pe.wait_ge(S["xf"].sem, S["xf"].at(n, 1))
                ps = mfill(n, "h4")
                mm(ps[0:FC, 0:T], xf[:], lpT[:], start=True, stop=True).then_inc(S["h4"].sem, 1)

            def f2(n):
                pe.wait_ge(S["g5"].sem, S["g5"].at(n, 1))
                ps = mfill(n, "f2")
                for q in range(QT):
                    last = mm(ps[:, q * D:(q + 1) * D], g5[:, q * P:(q + 1) * P], fc2_sb[:], start=True, stop=True)
                last.then_inc(S["f2"].sem, 1)

            def t_nC(n):
                pe.wait_ge(S["nc", "nrm"].sem, S["nc", "nrm"].at(n, QT))
                transposes(n, "nCT", "nCTmm", nC, QT, P, C)

            def s2(n):
                pe.wait_ge(S["nCT"].sem, S["nCT"].at(n, 1))
                ps = mfill(n, "s2")
                for q in range(QT):
                    for c in range(C):
                        last = mm(ps[:, q * T:(q + 1) * T], nCT[:, c, q * P:(q + 1) * P], nCT[:, c, :], start=(c == 0), stop=(c == C - 1))
                last.then_inc(S["s2"].sem, 1)

            def t_p2(n):
                pe.wait_ge(S["sp2"].sem, S["sp2"].at(n, QT))
                transposes(n, "p2T", "p2Tmm", sp2, QT, P, QT)

            def pv2(n):
                pe.wait_ge(S["p2T"].sem, S["p2T"].at(n, 1))
                ps = mfill(n, "pv2")
                for q in range(QT):
                    for kt in range(QT):
                        last = mm(ps[:, q * D:(q + 1) * D], p2T[:, kt, q * P:(q + 1) * P], nC[:, kt, :], start=(kt == 0), stop=(kt == QT - 1))
                last.then_inc(S["pv2"].sem, 1)

            run(pe, {"T": transposed, "cT": ctx_transposed, "qk": qk, "v": v, "pack": pack, "S": scores, "maxT": maxT, "E": shifted,
                     "pv": pv, "wo": wo, "gu": gu, "dn": dn, "nFT": t_nF, "nXT": t_nX, "sc": sc, "pT": pT, "h4": h4, "f2": f2,
                     "nCT": t_nC, "s2": s2, "p2T": t_p2, "pv2": pv2})


def kernel(**inputs):
    import numpy as np
    import concourse.bacc as bacc
    from concourse.bass_utils import run_bass_kernel_spmd

    L0 = lambda n: np.ascontiguousarray(inputs[f"L0_xattn_{n}"])
    L1 = lambda n: np.ascontiguousarray(inputs[f"L1_xattn_{n}"])
    arrays = {
        "x": np.ascontiguousarray(inputs["x"]), "ctx": np.ascontiguousarray(inputs["ctx_1024"]),
        "vecs": np.stack([L1(n) for n in ("norm1_w", "norm1_b", "norm2_w", "norm2_b", "norm3_w", "norm3_b", "gamma1", "gamma2")]),
        "norm_w": np.ascontiguousarray(np.concatenate([L0(n).reshape(C, P) for n in ("sa_norm_w", "ca_norm_w", "mlp_norm_w")]).T),
        "fc1t": np.ascontiguousarray(L1("fc1_w").T), "fc1b": L1("fc1_b"),
        "fc2t": np.ascontiguousarray(L1("fc2_w").T), "fc2b": L1("fc2_b"),
    }
    names = {n: n for n in ATTN_W} | {"gate": "w_gate", "up": "w_up", "down": "w_down"}
    for n, m in names.items():
        arrays[f"w_{n}"] = L0(m)
    nc = bacc.Bacc("TRN2", target_bir_lowering=False, num_devices=1)
    ap = {n: nc.dram_tensor(n, a.shape, mybir.dt.from_np(a.dtype), kind="ExternalInput").ap() for n, a in arrays.items()}
    out = nc.dram_tensor("out", (B, T, D), F32, kind="ExternalOutput").ap()
    build(nc, ap["x"], ap["ctx"], {n: ap[f"w_{n}"] for n in names}, ap["vecs"], ap["norm_w"], ap["fc1t"], ap["fc1b"],
          ap["fc2t"], ap["fc2b"], out)
    r = run_bass_kernel_spmd(nc, [arrays], core_ids=[0])
    return r.results[0]["out"]
```

```python
from contextlib import ExitStack

import concourse.bass as bass
from concourse import mybir

F32 = mybir.dt.float32
F32R = mybir.dt.float32r
ALU = mybir.AluOpType
ACT = mybir.ActivationFunctionType
AX_X = mybir.AxisListType.X

P = 128
B, T, D = 16, 256, 256
SKV = 77
SKV2 = SKV + 1
NH, HD = 16, 16
INNER = 1024
FC = 4
C = D // P
QT = T // P
M = INNER // P
PAIRS = 4
RMS_EPS = 1e-6
LN_EPS = 1e-5
HEAD_SCALE = HD ** -0.5
L1_SCALE = D ** -0.5
PARTS = ((0, 0), (0, 1), (1, 0))

ATTN_W = ["sa_wq", "sa_wk", "sa_wv", "sa_wo", "ca_wq", "ca_wk", "ca_wv", "ca_wo"]
ROWS = ["n1w", "n1b", "n2w", "n2b", "n3w", "n3b", "g1", "g2"]

PREPARE = ("norm", "ms", "xn", "T", "qk", "v", "pack")
L1_KINDS = ("lnstat", "lncen", "out", "nFT", "sc", "sce", "scn", "s2e", "pT", "h4", "f2", "nCT", "s2", "p2T", "pv2")
ITERATION = [
    ("norm", "mlp"), ("norm", "ca"), ("S", "sa", 0), ("ms", "mlp"), ("S", "sa", 1), ("xn", "mlp"), ("S", "sa", 2), ("ms", "ca"), ("S", "sa", 3),
    ("T", "mlp"), ("xn", "ca"), ("lnstat", "nf"), ("cT", "ca"), ("maxsplit", "sa", 0), ("S", "sa", 4), ("lncen", "nf"), ("gu", 0), ("T", "ca"),
    ("maxT", "sa", 0), ("gu", 1), ("S", "sa", 5), ("hi", 0), ("E", "sa", 0), ("gu", 2), ("hi", 1), ("gu", 3), ("E", "sa", 1), ("S", "sa", 6),
    ("nFT",), ("dnp", 0), ("S", "sa", 7), ("maxsplit", "sa", 1), ("sc",), ("dnp", 1), ("E", "sa", 2), ("E", "sa", 3), ("pv", "sa", 0), ("sce",),
    ("hi", 2), ("maxT", "sa", 1), ("scn",), ("qk", "ca"), ("pv", "sa", 1), ("pT",), ("E", "sa", 4), ("E", "sa", 5), ("at", "sa", 0), ("E", "sa", 6),
    ("lnstat", "nx"), ("E", "sa", 7), ("dnp", 2), ("lncen", "nx"), ("h4",), ("pv", "sa", 2), ("f2",), ("pv", "sa", 3), ("lnstat", "nc"), ("v", "ca"),
    ("at", "sa", 1), ("lncen", "nc"), ("pack", "ca", 0), ("wo", "sa"), ("hi", 3), ("gu", 4), ("nCT",), ("dnp", 3), ("hi", 4), ("pack", "ca", 1),
    ("nXT",), ("s2",), ("dnp", 4), ("norm", "sa"), ("ms", "sa"), ("s2e",), ("gu", 5), ("S", "ca", 0), ("p2T",), ("S", "ca", 1), ("xn", "sa"),
    ("maxsplit", "ca", 0), ("hi", 5), ("gu", 6), ("S", "ca", 2), ("S", "ca", 3), ("dnp", 5), ("maxsplit", "ca", 1), ("maxT", "ca", 0), ("pv2",),
    ("hi", 6), ("T", "sa"), ("maxT", "ca", 1), ("gu", 7), ("E", "ca", 0), ("E", "ca", 1), ("dnp", 6), ("hi", 7), ("out",), ("E", "ca", 2),
    ("pv", "ca", 0), ("E", "ca", 3), ("at", "ca", 0), ("qk", "sa"), ("dnp", 7), ("pv", "ca", 1), ("v", "sa"), ("dn",), ("at", "ca", 1),
    ("pack", "sa", 0), ("pack", "sa", 1), ("wo", "ca"), ("h1",),
]
LAG = 3


def track(step):
    if step[-1] in ("mlp", "nx") or step[0] in ("gu", "hi", "dnp", "dn", "nXT"):
        return 1 - LAG
    if step[0] in L1_KINDS:
        return -LAG
    if "ca" in step:
        return -1
    return 1 if step[0] in PREPARE and step[1] == "sa" else 0


def fills_of(step):
    if step[0] == "T" and step[1] == "mlp":
        return [], ["mT"]
    if step[0] in ("T", "qk", "v", "wo", "cT"):
        return [(step[1], step[0])], []
    if step[0] in ("S", "E", "maxT"):
        return [(step[1], step[0], step[2])], []
    if step[0] == "pack":
        _, tag, c = step
        return [(tag, "pq", c)] + ([(tag, "pk", c)] if tag == "sa" or c == 0 else []), []
    if step[0] == "gu":
        return [], [f"gu{step[1]}"]
    return [], [step[0]] if step[0] in ("nFT", "nXT", "sc", "pT", "h4", "f2", "nCT", "s2", "p2T", "pv2") else []


A_FILLS = [f for step in ITERATION for f in fills_of(step)[0]]
M_FILLS = [f for step in ITERATION for f in fills_of(step)[1]]
A_AHEAD = [track(step) for step in ITERATION for f in fills_of(step)[0]]
M_AHEAD = [track(step) for step in ITERATION for f in fills_of(step)[1]]


class Signal:

    def __init__(self, sem, per):
        self.sem, self.per = sem, per

    def at(self, n, j):
        return n * self.per + j


def not_first(n, back=1):
    return not isinstance(n, int) or n >= back


def sa_before_ca(n):
    return n + 1 if not isinstance(n, int) or n + 1 < B else n


def build(nc, x, ctx, w, vecs, norm_w, fc1t, fc1b, fc2t, fc2b, out):
    st = ExitStack()
    with st:
        def sb(name, shape, dt=F32):
            return st.enter_context(nc.sbuf_tensor(name, shape, dt))

        def sem(name):
            return st.enter_context(nc.semaphore(name))

        def sig(name, per):
            return Signal(sem(name), per)

        wt = {n: [sb(f"{n}_{p}", [P, C, D], F32R) for p in ("hi", "lo")] for n in ATTN_W}
        for n in ("gate", "up"):
            wt[n] = [sb(f"{n}_{p}", [P, C, INNER], F32R) for p in ("hi", "lo")]
        wt["down"] = [sb(f"down_{p}", [P, M, D], F32R) for p in ("hi", "lo")]
        W_ORDER = ATTN_W + ["gate", "up", "down"]
        normw = sb("normw", [P, 3, C])
        NORM_AT = {"sa": 0, "ca": 1, "mlp": 2}
        bc = sb("bc", [P, len(ROWS), D])
        fc1t_sb = sb("fc1t_sb", [P, C, FC])
        fc1b_sb = sb("fc1b_sb", [FC, 1])
        fc2_sb = sb("fc2_sb", [FC + 1, D])
        ident = sb("ident", [P, P])
        half_neg = sb("half_neg", [P, QT])
        ones_pad = sb("ones_pad", [P, 2, 32])
        sel = sb("sel", [P, 4, PAIRS, P], F32R)
        key_sel = sb("key_sel", [P, PAIRS])
        x_sb = sb("x_sb", [P, QT, D])
        ctx_sb = sb("ctx_sb", [SKV, D])
        h1 = sb("h1", [P, QT, D])
        h1_ca = sb("h1_ca", [P, QT, D])
        h2 = sb("h2", [P, QT, D])
        ss = {t: sb(f"{t}_sumsq", [P, QT]) for t in NORM_AT}
        ms = {t: sb(f"{t}_meansq", [P, QT]) for t in NORM_AT}
        rstd = {t: sb(f"{t}_rstd", [P, QT]) for t in NORM_AT}
        xn_a = sb("xn_a", [P, QT, D])
        xn_m = sb("xn_m", [P, QT, D])
        hT_a = [sb(f"hT_a_{p}", [P, C, T], F32R) for p in ("hi", "lo")]
        hT_m = [sb(f"hT_m_{p}", [P, C, T], F32R) for p in ("hi", "lo")]
        cT = [sb(f"cT_{p}", [P, C, SKV2], F32R) for p in ("hi", "lo")]
        qT = [sb(f"qT_{p}", [P, C, T], F32R) for p in ("hi", "lo")]
        kT = [sb(f"kT_{p}", [P, C, T], F32R) for p in ("hi", "lo")]
        qpk = sb("qpk", [P, 2 * PAIRS, T], F32R)
        kpk = sb("kpk", [P, 2, 2 * PAIRS, T], F32R)
        vz = sb("vz", [P, QT, NH, 32])
        GRANULES = 2
        probs = sb("probs", [P, GRANULES, PAIRS, 2, T])
        mx = sb("mx", [P, C, QT, 8])
        nm = sb("nm", [P, C, QT, 80])
        rD = sb("rD", [P, T])
        at = xn_a
        atT = [sb(f"atT_{p}", [P, C, T], F32R) for p in ("hi", "lo")]
        hid = sb("hid", [P, 2, T])
        HID = 3
        hidT = [sb(f"hidT_{p}", [P, HID, T], F32R) for p in ("hi", "lo")]
        ctx_l = sb("ctx_l", [SKV, 1, D])
        buf = [sb(f"l1_buf{i}", [P, QT, D]) for i in range(5)]
        h3 = sb("h3", [P, QT, D])
        cross = buf[0]
        nF, nC, sp2 = buf[1], buf[2], buf[3]
        t1 = buf[3]
        nFT = nCT = p2T = buf[4]
        o_sb = sb("o_sb", [P, QT, D])
        row_of = lambda k: buf[k // QT][0:1, k % QT, :]
        LN = {"nf": (P, QT, 2), "nx": (SKV, 1, 0), "nc": (P, QT, 4)}
        NRM = {"nf": nF, "nx": ctx_l, "nc": nC}
        stats = {t: sb(f"{t}_stats", [r, q, 6]) for t, (r, q, _) in LN.items()}
        mv = {t: sb(f"{t}_mv", [r, q, 2]) for t, (r, q, _) in LN.items()}
        ve = {t: sb(f"{t}_ve", [r, q]) for t, (r, q, _) in LN.items()}
        rs = {t: sb(f"{t}_rs", [r, q]) for t, (r, q, _) in LN.items()}
        nXT = sb("nXT", [P, C, SKV])
        lmx = sb("lmx", [P, QT])
        lnm = sb("lnm", [P, QT])
        lp = sb("lp", [P, QT, SKV])
        lsum = sb("lsum", [P, QT])
        lrec = sb("lrec", [P, QT])
        lpT = sb("lpT", [SKV, T])
        xf = sb("xf", [SKV, FC])
        g5 = sb("g5", [FC + 1, T])
        ones_row = g5[0:1, 0:P]
        smx = sb("smx", [P, QT])
        snm = sb("snm", [P, QT])
        ssum = sb("ssum", [P, QT])
        srec = sb("srec", [P, QT])

        ring = [st.enter_context(nc.psum_tensor(f"ring{i}", [P, 2, 512], F32)) for i in range(2)]
        down_ps = st.enter_context(nc.psum_tensor("down_ps", [P, QT, D], F32))
        od = st.enter_context(nc.psum_tensor("od", [P, 2, T], F32))
        mring = [st.enter_context(nc.psum_tensor(f"mring{i}", [P, 512], F32)) for i in range(2)]

        s_w = {n: sem(f"w_loaded_{n}") for n in W_ORDER}
        s_small = sem("small_loaded")
        N_SMALL = 5 + len(ROWS) // QT
        s_whi = sem("weights_hi")
        s_wlo = sem("weights_lo")
        s_cz = sem("const_zeroed")
        s_cset = sem("const_set")
        s_vset = sem("const_vector_set")
        s_bcmm = sem("rows_broadcast_mm")
        s_bc = sem("rows_broadcast")
        x_in = sig("x_in", 16)
        c_in = sig("ctx_in", 16)
        cl_in = sig("ctx_l_in", 16)
        stored = sig("stored", 16)
        S = {}
        for t in ("sa", "ca", "mlp"):
            for k, per in (("ss", QT), ("ms", 1), ("rstd", 1), ("xn", QT), ("T", 1), ("hi", C), ("lo", C)):
                S[t, k] = sig(f"{t}_{k}", per)
        for t, fills in (("sa", 8), ("ca", 4)):
            for k, per in (("qkmm", 1), ("qkhi", 2), ("qklo", 2), ("vmm", 1), ("vz", 2), ("pqmm", 2), ("pkmm", 2 if t == "sa" else 1),
                           ("pq", 2), ("pk", 4), ("S", fills), ("mx", 8), ("nm", 8),
                           ("maxT", 2), ("maxrows", 4), ("E", fills), ("exp", fills), ("pv", 4 if t == "sa" else 2), ("rD", 2),
                           ("at", 2), ("athi", 2), ("atlo", 2), ("wo", 1), ("res", 1)):
                S[t, k] = sig(f"{t}_{k}", per)
        for k, per in (("cTmm", 1), ("cThi", 1), ("cTlo", 1)):
            S[k] = sig(k, per)
        for k, per in (("gu", M), ("tanh", M), ("ga", M), ("hid", M), ("hidhi", M), ("hidlo", M), ("dnp", M), ("h1", 1), ("h3", 1),
                       ("nFTmm", 1), ("nFT", 1), ("nXTmm", 1), ("nXT", 1), ("scmm", 1), ("lmx", 1), ("lnm", 1),
                       ("lp", QT), ("xf", 1), ("lrec", 1), ("lpn", QT), ("pTmm", 1), ("lpT", 1), ("h4", 1), ("g5", 1),
                       ("f2", 1), ("cross", 1), ("nCTmm", 1), ("nCT", 1), ("s2", 1), ("smx", 1), ("snm", 1),
                       ("sp2", QT), ("srec", 1), ("p2Tmm", 1), ("p2T", 1), ("pv2", 1), ("t1", QT), ("t2", QT),
                       ("t3", QT), ("o", QT)):
            S[k] = sig(k, per)
        for t, (_, q, _) in LN.items():
            for k, per in (("st", q), ("mv", q), ("ve", 1), ("rs", 1), ("cen", q), ("scl", q), ("nrm", q)):
                S[t, k] = sig(f"{t}_{k}", per)

        STAGE_COL = [512 * k for k in range(8)] + [0, 2048, 0]
        STAGE_AFTER = [0] * 8 + [4, 8, 9]

        def stage_of(k):
            cols = 512 if k < len(ATTN_W) else 2048
            return probs[:].rearrange("p g i h t -> p (g i h t)")[:, STAGE_COL[k]:STAGE_COL[k] + cols]

        def freed(name):
            if isinstance(name, str):
                if name.startswith("gu"):
                    return S["hid"], int(name[2:]) + 1
                return {"mT": (S["mlp", "lo"], C), "nFT": (S["nFT"], 1), "nXT": (S["nXT"], 1),
                        "sc": (S["xf"], 1), "pT": (S["lpT"], 1), "h4": (S["g5"], 1), "f2": (S["cross"], 1),
                        "nCT": (S["nCT"], 1), "s2": (S["sp2"], QT), "p2T": (S["p2T"], 1), "pv2": (S["t1"], QT)}[name]
            tag, kind, k = (*name, 0)[:3]
            return {"T": lambda: (S[tag, "lo"], C), "qk": lambda: (S[tag, "qklo"], 2), "v": lambda: (S[tag, "vz"], 2),
                    "pq": lambda: (S[tag, "pq"], k + 1), "pk": lambda: (S[tag, "pk"], 2 * (k + 1) if tag == "sa" else 4),
                    "S": lambda: (S[tag, "mx"], (k + 1) * (1 if tag == "sa" else 2)),
                    "E": lambda: (S[tag, "exp"], k + 1), "wo": lambda: (S[tag, "res"], 1),
                    "cT": lambda: (S["cTlo"], 1), "maxT": lambda: (S[tag, "maxrows"], 2 * (k + 1))}[kind]()

        def ring_tile(name):
            return ring[A_FILLS.index(name) % 2]

        def mring_tile(name):
            return mring[M_FILLS.index(name) % 2]

        SPLIT = {t: (hT_m if t == "mlp" else hT_a) for t in NORM_AT}
        XN = {"sa": xn_a, "ca": xn_a, "mlp": xn_m}
        NORM_SRC = {"sa": x_sb, "ca": h1_ca, "mlp": h2}

        def wait_norm_source(eng, tag, n):
            if tag == "sa":
                eng.wait_ge(x_in.sem, x_in.at(n, 16))
            elif tag == "ca":
                eng.wait_ge(S["h1"].sem, S["h1"].at(n, 1))
            else:
                eng.wait_ge(S["ca", "res"].sem, S["ca", "res"].at(n, 1))

        def norm_tile(tag):
            return mring_tile("mT") if tag == "mlp" else ring_tile((tag, "T"))[:, 0, :]

        def pair_head(k, tag):
            return (k // 4, k % 4, 1) if tag == "sa" else (k // 2, 2 * (k % 2), 2)

        def shifted_at(k, tag):
            tiles = QT if tag == "sa" else 1
            return k // (2 * tiles), (k // 2) % tiles, 2 * (k % 2), k // 2

        def granule(g, tag):
            return probs[:, g % GRANULES]

        def run(eng, todo):
            def one(it):
                for step in ITERATION:
                    f, n = todo.get(step[0]), it + track(step)
                    if f and (not isinstance(n, int) or 0 <= n < B):
                        f(n, *step[1:])

            for it in range(-1, LAG + 1):
                one(it)
            with eng.Fori(LAG + 1, B - 1) as it:
                one(it)
            for it in range(B - 1, B + LAG):
                one(it)

        block = st.enter_context(nc.Block())

        @block.sync
        def _(sp):
            x_v = x.rearrange("b (q p) d -> b p q d", p=P)
            o_v = out.rearrange("b (q p) d -> b p q d", p=P)
            sp.dma_start(x_sb[:], x_v[0]).then_inc(x_in.sem, 16)
            sp.dma_start(normw[:].rearrange("p n c -> p (n c)"), norm_w).then_inc(s_small, 16)
            for k in range(0, len(ROWS), QT):
                sp.dma_start(buf[k // QT][0:1, :, :], vecs[k:k + QT, :].rearrange("(o n) d -> o n d", o=1)).then_inc(s_small, 16)
            sp.dma_start(fc1t_sb[:], fc1t.rearrange("(c p) h -> p c h", p=P)).then_inc(s_small, 16)
            sp.dma_start(fc1b_sb[:], fc1b.rearrange("(h o) -> h o", o=1)).then_inc(s_small, 16)
            sp.dma_start(fc2_sb[0:FC, :], fc2t).then_inc(s_small, 16)
            sp.dma_start(fc2_sb[FC:FC + 1, :], fc2b.rearrange("(o d) -> o d", o=1)).then_inc(s_small, 16)
            for k, n in enumerate(W_ORDER):
                if STAGE_AFTER[k]:
                    sp.wait_ge(s_wlo, STAGE_AFTER[k])
                sp.dma_start(stage_of(k).rearrange("p (c n) -> p c n", n=w[n].shape[1]),
                             w[n].rearrange("(c p) n -> p c n", p=P)).then_inc(s_w[n], 16)
            sp.dma_start(ctx_sb[:], ctx[0]).then_inc(c_in.sem, 16)

            def load_x(n):
                if not_first(n):
                    sp.wait_ge(S["sa", "res"].sem, S["sa", "res"].at(n - 1, 1))
                sp.dma_start(x_sb[:], x_v[n]).then_inc(x_in.sem, 16)

            def load_ctx(n):
                if not_first(n):
                    sp.wait_ge(S["cTmm"].sem, S["cTmm"].at(n - 1, 1))
                sp.dma_start(ctx_sb[:], ctx[n]).then_inc(c_in.sem, 16)

            def load_ctx_l(n):
                if not_first(n):
                    sp.wait_ge(S["nXTmm"].sem, S["nXTmm"].at(n - 1, 1))
                sp.dma_start(ctx_l[:, 0, :], ctx[n]).then_inc(cl_in.sem, 16)

            def store(n):
                sp.wait_ge(S["o"].sem, S["o"].at(n, QT))
                sp.dma_start(o_v[n], o_sb[:]).then_inc(stored.sem, 16)

            def iteration(it):
                if not isinstance(it, int) or 0 <= it - LAG + 1 < B:
                    load_ctx_l(it - LAG + 1)
                if not isinstance(it, int) or 1 <= it < B:
                    load_ctx(it)
                if not isinstance(it, int) or 0 <= it < B - 1:
                    load_x(it + 1)
                if not isinstance(it, int) or 0 <= it - LAG < B:
                    store(it - LAG)

            for it in range(LAG + 1):
                iteration(it)
            with sp.Fori(LAG + 1, B - 1) as it:
                iteration(it)
            for it in range(B - 1, B + LAG):
                iteration(it)
            sp.wait_ge(stored.sem, stored.at(B - 1, 16))

        @block.gpsimd
        def _(pool):
            nc.gpsimd.memset(ident[:], 0.0).then_inc(s_cz, 1)
            nc.gpsimd.memset(sel[:].bitcast(F32), 0.0).then_inc(s_cz, 1)
            nc.gpsimd.memset(key_sel[:], 0.0).then_inc(s_cz, 1)
            pool.wait_ge(s_cz, 3)
            nc.gpsimd.affine_select(out=ident[:], in_=ident[:], compare_op=ALU.not_equal, fill=1.0, base=0,
                                    pattern=[[-1, P]], channel_multiplier=1).then_inc(s_cset, 1)
            for kind, r0, step in ((0, 1, 2), (1, 2, 0), (2, 1, 1), (3, 3, 0)):
                for i in range(PAIRS):
                    v = sel[:, kind, i, :].rearrange("p (h r d) -> p h r d", h=2, r=4)[:, :, r0:r0 + step + 1:max(step, 1), :]
                    nc.gpsimd.affine_select(out=v, in_=v.bitcast(F32), compare_op=ALU.not_equal, fill=1.0, base=-32 * i,
                                            pattern=[[-16, 2], [0, 2 if step else 1], [-1, 16]], channel_multiplier=1).then_inc(s_cset, 1)
            for part, base in enumerate((0, 8, 64 + 1, 64 + 8 + 1)):
                if part:
                    pool.wait_ge(s_cset, 1 + 4 * PAIRS + part)
                nc.gpsimd.affine_select(out=key_sel[:], in_=key_sel[:], compare_op=ALU.not_equal, fill=1.0,
                                        base=-base, pattern=[[-2, PAIRS]], channel_multiplier=1).then_inc(s_cset, 1)

            def rstds(n, tag):
                pool.wait_ge(S[tag, "ms"].sem, S[tag, "ms"].at(n, 1))
                nc.gpsimd.tensor_tensor(rstd[tag][:], ms[tag][:], half_neg[:], ALU.pow).then_inc(S[tag, "rstd"].sem, 1)

            def normalised(n, tag, c):
                pool.wait_ge(S[tag, "athi"].sem, S[tag, "athi"].at(n, c + 1))
                nc.gpsimd.tensor_tensor(atT[1][:, c, :], at[:, c, :], atT[0][:, c, :].bitcast(F32), ALU.subtract).then_inc(S[tag, "atlo"].sem, 1)

            def hid_lo(n, m):
                pool.wait_ge(S["hidhi"].sem, S["hidhi"].at(n, m + 1))
                nc.gpsimd.tensor_tensor(hidT[1][:, m % HID, :], hid[:, m % 2, :], hidT[0][:, m % HID, :].bitcast(F32), ALU.subtract).then_inc(S["hidlo"].sem, 1)

            def lnstat(n, tag):
                r, tiles, _ = LN[tag]
                pool.wait_ge(S[tag, "ve"].sem, S[tag, "ve"].at(n, 1))
                nc.gpsimd.tensor_tensor(rs[tag][:], ve[tag][:], half_neg[0:r, 0:tiles], ALU.pow).then_inc(S[tag, "rs"].sem, 1)

            def lncen(n, tag):
                r, tiles, at_row = LN[tag]
                for q in range(tiles):
                    pool.wait_ge(S[tag, "cen"].sem, S[tag, "cen"].at(n, q + 1))
                    nc.gpsimd.tensor_tensor(NRM[tag][:, q, :], NRM[tag][:, q, :], bc[0:r, at_row, :], ALU.mult).then_inc(S[tag, "scl"].sem, 1)
                for q in range(tiles):
                    pool.wait_ge(S[tag, "scl"].sem, S[tag, "scl"].at(n, q + 1))
                    nc.gpsimd.tensor_tensor(NRM[tag][:, q, :], NRM[tag][:, q, :], bc[0:r, at_row + 1, :], ALU.add).then_inc(S[tag, "nrm"].sem, 1)

            def out_(n):
                for q in range(QT):
                    pool.wait_ge(S["t1"].sem, S["t1"].at(n, q + 1))
                    nc.gpsimd.tensor_tensor(t1[:, q, :], t1[:, q, :], cross[:, q, :], ALU.add).then_inc(S["t2"].sem, 1)
                for q in range(QT):
                    pool.wait_ge(S["t2"].sem, S["t2"].at(n, q + 1))
                    nc.gpsimd.tensor_tensor(t1[:, q, :], t1[:, q, :], bc[:, 7, :], ALU.mult).then_inc(S["t3"].sem, 1)
                if not_first(n):
                    pool.wait_ge(stored.sem, stored.at(n - 1, 16))
                for q in range(QT):
                    pool.wait_ge(S["t3"].sem, S["t3"].at(n, q + 1))
                    nc.gpsimd.tensor_tensor(o_sb[:, q, :], t1[:, q, :], nF[:, q, :], ALU.add).then_inc(S["o"].sem, 1)

            pool.wait_ge(s_bc, 2)
            pool.wait_ge(s_vset, 1)
            run(pool, {"ms": rstds, "at": normalised, "hi": hid_lo, "lnstat": lnstat, "lncen": lncen, "out": out_})

        @block.scalar
        def _(act):
            for k, n in enumerate(W_ORDER):
                act.wait_ge(s_w[n], 16)
                nc.scalar.activation(wt[n][0][:].rearrange("p c n -> p (c n)"), stage_of(k), ACT.Copy).then_inc(s_whi, 1)
            act.wait_ge(s_bcmm, 1)
            for b in range(2):
                nc.scalar.activation(bc[:, 4 * b:4 * b + 4, :], ring[b][:].rearrange("p b (r d) -> p (b r) d", d=D), ACT.Copy).then_inc(s_bc, 1)
            act.wait_ge(s_small, 16 * N_SMALL)
            act.wait_ge(s_wlo, len(W_ORDER))

            def h1_for_ca(n):
                act.wait_ge(S["sa", "res"].sem, S["sa", "res"].at(n, 1))
                if not_first(n):
                    act.wait_ge(S["ca", "res"].sem, S["ca", "res"].at(n - 1, 1))
                nc.scalar.activation(h1_ca[:], h1[:], ACT.Copy).then_inc(S["h1"].sem, 1)

            def norm(n, tag):
                wait_norm_source(act, tag, n)
                for q in range(QT):
                    nc.scalar.activation(XN[tag][:, q, :], NORM_SRC[tag][:, q, :], ACT.Square,
                                         accum_out=ss[tag][:, q:q + 1]).then_inc(S[tag, "ss"].sem, 1)

            def transposed(n, tag):
                act.wait_ge(S[tag, "T"].sem, S[tag, "T"].at(n, 1))
                ps = norm_tile(tag)
                for c in range(C):
                    nc.scalar.activation(SPLIT[tag][0][:, c, :], ps[:, c * T:(c + 1) * T], ACT.Copy,
                                         scale=normw[:, NORM_AT[tag], c:c + 1]).then_inc(S[tag, "hi"].sem, 1)

            def ctx_transposed(n, tag):
                act.wait_ge(S["cTmm"].sem, S["cTmm"].at(n, 1))
                ps = ring_tile(("ca", "cT"))[:, 0, 0:C * SKV].rearrange("p (c t) -> p c t", c=C)
                nc.scalar.activation(cT[0][:, :, 0:SKV], ps, ACT.Copy).then_inc(S["cThi"].sem, 1)

            def qk(n, tag):
                act.wait_ge(S[tag, "qkmm"].sem, S[tag, "qkmm"].at(n, 1))
                ps = ring_tile((tag, "qk"))
                kw = T if tag == "sa" else SKV2
                nc.scalar.activation(qT[0][:], ps[:, 0, :].rearrange("p (c t) -> p c t", c=C), ACT.Copy).then_inc(S[tag, "qkhi"].sem, 1)
                nc.scalar.activation(kT[0][:, :, 0:kw], ps[:, 1, 0:C * kw].rearrange("p (c t) -> p c t", c=C), ACT.Copy).then_inc(S[tag, "qkhi"].sem, 1)

            def v(n, tag):
                act.wait_ge(S[tag, "vmm"].sem, S[tag, "vmm"].at(n, 1))
                rows_, tiles = (P, QT) if tag == "sa" else (SKV, 1)
                ps = ring_tile((tag, "v"))[0:rows_, 0, 0:tiles * D].rearrange("p (k s h d) -> p k s h d", k=tiles, h=2, d=HD)
                vv = vz[0:rows_, 0:tiles].rearrange("p k (s h) e -> p k s h e", h=2)
                for half in range(2):
                    nc.scalar.activation(vv[:, :, :, half, half * HD:(half + 1) * HD], ps[:, :, :, half, :], ACT.Copy).then_inc(S[tag, "vz"].sem, 1)

            def pack(n, tag, c):
                act.wait_ge(S[tag, "pqmm"].sem, S[tag, "pqmm"].at(n, c + 1))
                ps = ring_tile((tag, "pq", c))[:].rearrange("p b (s t) -> p (b s) t", t=T)
                nc.scalar.activation(qpk[:, PAIRS * c:PAIRS * (c + 1), :], ps, ACT.Copy).then_inc(S[tag, "pq"].sem, 1)

            def maxT(n, tag, c):
                act.wait_ge(S[tag, "maxT"].sem, S[tag, "maxT"].at(n, c + 1))
                for r0 in (0, 64):
                    ps = ring_tile((tag, "maxT", c))[r0:r0 + 16, 0:1, 0:T].to_broadcast([16, PAIRS, T])
                    nc.scalar.activation(qpk[r0:r0 + 16, PAIRS * c:PAIRS * (c + 1), :], ps, ACT.Copy).then_inc(S[tag, "maxrows"].sem, 1)

            def exps(n, tag, k):
                act.wait_ge(S[tag, "E"].sem, S[tag, "E"].at(n, k + 1))
                c, kt, i0, g = shifted_at(k, tag)
                if k % 2 == 0:
                    if g >= GRANULES:
                        act.wait_ge(S[tag, "pv"].sem, S[tag, "pv"].at(n, g - GRANULES + 1))
                    elif tag == "ca":
                        act.wait_ge(S["sa", "pv"].sem, S["sa", "pv"].at(sa_before_ca(n), 4 - GRANULES + g + 1))
                    else:
                        if not_first(n, 2):
                            act.wait_ge(S["ca", "pv"].sem, S["ca", "pv"].at(n - 2, 2 - GRANULES + g + 1))
                rows_ = P if tag == "sa" else SKV
                nc.scalar.activation(granule(g, tag)[0:rows_, i0:i0 + 2, :, :].rearrange("p i h t -> p h i t"),
                                     ring_tile((tag, "E", k))[0:rows_].rearrange("p h (i t) -> p h i t", t=T),
                                     ACT.Exp, scale=HEAD_SCALE).then_inc(S[tag, "exp"].sem, 1)

            def normalised(n, tag, c):
                act.wait_ge(S[tag, "at"].sem, S[tag, "at"].at(n, c + 1))
                nc.scalar.activation(atT[0][:, c, :], at[:, c, :], ACT.Copy).then_inc(S[tag, "athi"].sem, 1)

            def gu(n, m):
                act.wait_ge(S["gu"].sem, S["gu"].at(n, m + 1))
                if m >= 2:
                    act.wait_ge(S["hidlo"].sem, S["hidlo"].at(n, m - 1))
                nc.scalar.activation(hid[:, m % 2, :], mring_tile(f"gu{m}")[:, 0:T], ACT.Tanh, scale=0.5).then_inc(S["tanh"].sem, 1)

            def hid_hi(n, m):
                act.wait_ge(S["hid"].sem, S["hid"].at(n, m + 1))
                if m >= HID:
                    act.wait_ge(S["dnp"].sem, S["dnp"].at(n, m - HID + 1))
                elif not_first(n):
                    act.wait_ge(S["dnp"].sem, S["dnp"].at(n - 1, M))
                nc.scalar.activation(hidT[0][:, m % HID, :], hid[:, m % 2, :], ACT.Copy).then_inc(S["hidhi"].sem, 1)

            def evacuate(signal, done, fill, dst, rows_, cols):
                def f(n):
                    act.wait_ge(S[signal].sem, S[signal].at(n, 1))
                    nc.scalar.activation(dst, mring_tile(fill)[0:rows_, 0:cols], ACT.Copy).then_inc(S[done].sem, 1)
                return f

            def sce(n):
                act.wait_ge(S["lnm"].sem, S["lnm"].at(n, 1))
                for q in range(QT):
                    nc.scalar.activation(lp[:, q, :], mring_tile("sc")[:, q * SKV:(q + 1) * SKV], ACT.Exp,
                                         bias=lnm[:, q:q + 1], scale=L1_SCALE, accum_out=lsum[:, q:q + 1]).then_inc(S["lp"].sem, 1)
                nc.scalar.activation(xf[:], mring_tile("sc")[0:SKV, QT * SKV:QT * SKV + FC], ACT.Copy).then_inc(S["xf"].sem, 1)

            def h4(n):
                act.wait_ge(S["h4"].sem, S["h4"].at(n, 1))
                nc.scalar.activation(g5[0:FC, :], mring_tile("h4")[0:FC, 0:T], ACT.Gelu, bias=fc1b_sb[:, 0:1]).then_inc(S["g5"].sem, 1)

            def s2e(n):
                act.wait_ge(S["snm"].sem, S["snm"].at(n, 1))
                for q in range(QT):
                    nc.scalar.activation(sp2[:, q, :], mring_tile("s2")[:, q * T:(q + 1) * T], ACT.Exp,
                                         bias=snm[:, q:q + 1], scale=L1_SCALE, accum_out=ssum[:, q:q + 1]).then_inc(S["sp2"].sem, 1)

            flat = lambda t: t[:].rearrange("p c t -> p (c t)")
            run(act, {"h1": h1_for_ca, "norm": norm, "T": transposed, "cT": ctx_transposed, "qk": qk, "v": v, "pack": pack, "maxT": maxT, "E": exps, "at": normalised, "gu": gu, "hi": hid_hi,
                      "nFT": evacuate("nFTmm", "nFT", "nFT", flat(nFT), P, C * T),
                      "nXT": evacuate("nXTmm", "nXT", "nXT", flat(nXT), P, C * SKV),
                      "sce": sce, "pT": evacuate("pTmm", "lpT", "pT", lpT[:], SKV, T), "h4": h4,
                      "f2": evacuate("f2", "cross", "f2", flat(cross), P, QT * D),
                      "nCT": evacuate("nCTmm", "nCT", "nCT", flat(nCT), P, C * T), "s2e": s2e,
                      "p2T": evacuate("p2Tmm", "p2T", "p2T", flat(p2T), P, QT * T)})

        @block.vector
        def _(dve):
            nc.vector.memset(half_neg[:], -0.5).then_inc(s_vset, 1)
            nc.vector.memset(vz[:], 0.0).then_inc(s_vset, 1)
            nc.vector.memset(g5[:], 1.0).then_inc(s_vset, 1)
            nc.vector.memset(kpk[:].bitcast(F32), 0.0).then_inc(s_vset, 1)
            for p in range(2):
                nc.vector.memset(cT[p][:].bitcast(F32), 0.0).then_inc(s_vset, 1)
            nc.vector.memset(ones_pad[:], 0.0).then_inc(s_vset, 1)
            nc.vector.memset(nm[:], 0.0).then_inc(s_vset, 1)
            dve.wait_ge(s_vset, 8)
            for half in range(2):
                nc.vector.memset(ones_pad[:, half, half * HD:(half + 1) * HD], 1.0).then_inc(s_vset, 1)
            for k, n in enumerate(W_ORDER):
                dve.wait_ge(s_whi, k + 1)
                hi, lo = (t[:].rearrange("p c n -> p (c n)") for t in wt[n])
                nc.vector.tensor_tensor(lo, stage_of(k), hi.bitcast(F32), ALU.subtract).then_inc(s_wlo, 1)

            def meansq(n, tag):
                dve.wait_ge(S[tag, "ss"].sem, S[tag, "ss"].at(n, QT))
                nc.vector.tensor_scalar(ms[tag][:], ss[tag][:], 1.0 / D, RMS_EPS, ALU.mult, ALU.add).then_inc(S[tag, "ms"].sem, 1)

            def xn(n, tag):
                dve.wait_ge(S[tag, "rstd"].sem, S[tag, "rstd"].at(n, 1))
                wait_norm_source(dve, tag, n)
                for q in range(QT):
                    nc.vector.tensor_scalar(XN[tag][:, q, :], NORM_SRC[tag][:, q, :], rstd[tag][:, q:q + 1], None, ALU.mult).then_inc(S[tag, "xn"].sem, 1)

            def transposed(n, tag):
                dve.wait_ge(S[tag, "hi"].sem, S[tag, "hi"].at(n, C))
                ps = norm_tile(tag)
                for c in range(C):
                    nc.vector.scalar_tensor_tensor(out=SPLIT[tag][1][:, c, :], in0=ps[:, c * T:(c + 1) * T],
                                                   scalar=normw[:, NORM_AT[tag], c:c + 1], in1=SPLIT[tag][0][:, c, :].bitcast(F32),
                                                   op0=ALU.mult, op1=ALU.subtract).then_inc(S[tag, "lo"].sem, 1)

            def ctx_transposed(n, tag):
                dve.wait_ge(S["cThi"].sem, S["cThi"].at(n, 1))
                ps = ring_tile(("ca", "cT"))[:, 0, 0:C * SKV].rearrange("p (c t) -> p c t", c=C)
                nc.vector.tensor_tensor(cT[1][:, :, 0:SKV], ps, cT[0][:, :, 0:SKV].bitcast(F32), ALU.subtract).then_inc(S["cTlo"].sem, 1)

            def qk(n, tag):
                ps = ring_tile((tag, "qk"))
                kw = T if tag == "sa" else SKV2
                dve.wait_ge(S[tag, "qkhi"].sem, S[tag, "qkhi"].at(n, 1))
                nc.vector.tensor_tensor(qT[1][:], ps[:, 0, :].rearrange("p (c t) -> p c t", c=C), qT[0][:].bitcast(F32), ALU.subtract).then_inc(S[tag, "qklo"].sem, 1)
                dve.wait_ge(S[tag, "qkhi"].sem, S[tag, "qkhi"].at(n, 2))
                nc.vector.tensor_tensor(kT[1][:, :, 0:kw], ps[:, 1, 0:C * kw].rearrange("p (c t) -> p c t", c=C),
                                        kT[0][:, :, 0:kw].bitcast(F32), ALU.subtract).then_inc(S[tag, "qklo"].sem, 1)

            def pack(n, tag, c):
                if tag == "sa":
                    dve.wait_ge(S[tag, "pkmm"].sem, S[tag, "pkmm"].at(n, c + 1))
                    ps = ring_tile((tag, "pk", c))[:].rearrange("p b (s t) -> p (b s) t", t=T)
                    for half in range(2):
                        r = slice(64 * half, 64 * half + 64)
                        nc.vector.tensor_tensor(kpk[r, half, PAIRS * c:PAIRS * (c + 1), :], ps[r],
                                                key_sel[r].rearrange("p (s o) -> p s o", o=1).to_broadcast([64, PAIRS, T]), ALU.add).then_inc(S[tag, "pk"].sem, 1)
                elif c == 0:
                    dve.wait_ge(S[tag, "pkmm"].sem, S[tag, "pkmm"].at(n, 1))
                    for cc in range(C):
                        for half in range(2):
                            r = slice(64 * half, 64 * half + 64)
                            ps = ring_tile((tag, "pk", 0))[r, cc, 0:PAIRS * SKV2].rearrange("p (s t) -> p s t", t=SKV2)
                            nc.vector.tensor_tensor(kpk[r, half, PAIRS * cc:PAIRS * (cc + 1), 0:SKV2], ps,
                                                    key_sel[r].rearrange("p (s o) -> p s o", o=1).to_broadcast([64, PAIRS, SKV2]), ALU.add).then_inc(S[tag, "pk"].sem, 1)

            def maxima(n, tag, k):
                dve.wait_ge(S[tag, "S"].sem, S[tag, "S"].at(n, k + 1))
                c, i, pairs = pair_head(k, tag)
                ps = ring_tile((tag, "S", k))
                if tag == "sa":
                    nc.vector.tensor_reduce(mx[:, c, :, 2 * i:2 * i + 2].rearrange("p q h -> p h q"),
                                            ps[:].rearrange("p h (q t) -> p h q t", t=T), AX_X, ALU.max).then_inc(S[tag, "mx"].sem, 1)
                else:
                    for half in range(2):
                        v = ps[:, half, 0:2 * QT * SKV2].rearrange("p (i q t) -> p i q t", i=2, t=SKV2)[:, :, :, 0:SKV]
                        nc.vector.tensor_reduce(mx[:, c, :, 2 * i + half:2 * i + half + 3:2].rearrange("p q i -> p i q"),
                                                v, AX_X, ALU.max).then_inc(S[tag, "mx"].sem, 1)

            def maxsplit(n, tag, c):
                dve.wait_ge(S[tag, "mx"].sem, S[tag, "mx"].at(n, 4 * (c + 1)))
                for at0 in (0, 64):
                    nc.vector.tensor_scalar(nm[:, c, :, at0:at0 + 8].bitcast(F32R), mx[:, c, :, :], -1.0, None, ALU.mult).then_inc(S[tag, "nm"].sem, 1)
                for k, at0 in enumerate((0, 64)):
                    dve.wait_ge(S[tag, "nm"].sem, S[tag, "nm"].at(n, 4 * c + k + 1))
                    nc.vector.scalar_tensor_tensor(out=nm[:, c, :, at0 + 8:at0 + 16], in0=mx[:, c, :, :], scalar=-1.0, in1=nm[:, c, :, at0:at0 + 8],
                                                   op0=ALU.mult, op1=ALU.subtract).then_inc(S[tag, "nm"].sem, 1)

            def normalise(n, tag, c):
                dve.wait_ge(S[tag, "pv"].sem, S[tag, "pv"].at(n, (QT if tag == "sa" else 1) * (c + 1)))
                nc.vector.reciprocal(rD[:], od[:, 1, :]).then_inc(S[tag, "rD"].sem, 1)
                dve.wait_ge(S[tag, "rD"].sem, S[tag, "rD"].at(n, c + 1))
                nc.vector.tensor_tensor(at[:, c, :], od[:, 0, :], rD[:], ALU.mult).then_inc(S[tag, "at"].sem, 1)

            def wo(n, tag):
                dve.wait_ge(S[tag, "wo"].sem, S[tag, "wo"].at(n, 1))
                src, dst = (x_sb, h1) if tag == "sa" else (h1_ca, h2)
                if tag == "sa" and not_first(n):
                    dve.wait_ge(S["h1"].sem, S["h1"].at(n - 1, 1))
                if tag == "ca" and not_first(n):
                    dve.wait_ge(S["h3"].sem, S["h3"].at(n - 1, 1))
                ps = ring_tile((tag, "wo"))[:, 0, :].rearrange("p (q d) -> p q d", q=QT)
                nc.vector.tensor_tensor(dst[:], src[:], ps, ALU.add).then_inc(S[tag, "res"].sem, 1)

            def gu(n, m):
                ps = mring_tile(f"gu{m}")
                dve.wait_ge(S["tanh"].sem, S["tanh"].at(n, m + 1))
                nc.vector.scalar_tensor_tensor(out=hid[:, m % 2, :], in0=hid[:, m % 2, :], scalar=1.0, in1=ps[:, 0:T], op0=ALU.add, op1=ALU.mult).then_inc(S["ga"].sem, 1)
                dve.wait_ge(S["ga"].sem, S["ga"].at(n, m + 1))
                nc.vector.scalar_tensor_tensor(out=hid[:, m % 2, :], in0=hid[:, m % 2, :], scalar=0.5, in1=ps[:, T:2 * T], op0=ALU.mult, op1=ALU.mult).then_inc(S["hid"].sem, 1)

            def dn(n):
                dve.wait_ge(S["dnp"].sem, S["dnp"].at(n, M))
                nc.vector.tensor_tensor(h3[:], h2[:], down_ps[:], ALU.add).then_inc(S["h3"].sem, 1)

            LN_SRC = {"nf": h3, "nx": ctx_l, "nc": cross}

            def lnstat(n, tag):
                r, tiles, _ = LN[tag]
                if tag == "nx":
                    dve.wait_ge(cl_in.sem, cl_in.at(n, 16))
                else:
                    dve.wait_ge(S[{"nf": "h3", "nc": "cross"}[tag]].sem, S[{"nf": "h3", "nc": "cross"}[tag]].at(n, 1))
                src = [LN_SRC[tag][:, q, :] for q in range(tiles)]
                for q in range(tiles):
                    nc.vector.bn_stats(stats[tag][:, q, :], src[q]).then_inc(S[tag, "st"].sem, 1)
                dve.wait_ge(S[tag, "st"].sem, S[tag, "st"].at(n, tiles))
                nc.vector.memset(ve[tag][:], LN_EPS)
                for q in range(tiles):
                    nc.vector.bn_aggr(mv[tag][:, q, :], stats[tag][:, q, :]).then_inc(S[tag, "mv"].sem, 1)
                dve.wait_ge(S[tag, "mv"].sem, S[tag, "mv"].at(n, tiles))
                nc.vector.tensor_tensor(ve[tag][:], ve[tag][:], mv[tag][:, :, 1], ALU.add).then_inc(S[tag, "ve"].sem, 1)

            def lncen(n, tag):
                src, tiles = LN_SRC[tag], LN[tag][1]
                dve.wait_ge(S[tag, "rs"].sem, S[tag, "rs"].at(n, 1))
                for q in range(tiles):
                    nc.vector.tensor_scalar(NRM[tag][:, q, :], src[:, q, :], mv[tag][:, q, 0:1], rs[tag][:, q:q + 1],
                                            ALU.subtract, ALU.mult).then_inc(S[tag, "cen"].sem, 1)

            def sc(n):
                dve.wait_ge(S["scmm"].sem, S["scmm"].at(n, 1))
                nc.vector.tensor_reduce(lmx[:], mring_tile("sc")[:, 0:QT * SKV].rearrange("p (q t) -> p q t", q=QT), AX_X, ALU.max).then_inc(S["lmx"].sem, 1)
                dve.wait_ge(S["lmx"].sem, S["lmx"].at(n, 1))
                nc.vector.tensor_scalar(lnm[:], lmx[:], -L1_SCALE, None, ALU.mult).then_inc(S["lnm"].sem, 1)

            def scn(n):
                dve.wait_ge(S["lp"].sem, S["lp"].at(n, QT))
                nc.vector.reciprocal(lrec[:], lsum[:]).then_inc(S["lrec"].sem, 1)
                dve.wait_ge(S["lrec"].sem, S["lrec"].at(n, 1))
                for q in range(QT):
                    nc.vector.tensor_scalar(lp[:, q, :], lp[:, q, :], lrec[:, q:q + 1], None, ALU.mult).then_inc(S["lpn"].sem, 1)

            def s2(n):
                dve.wait_ge(S["s2"].sem, S["s2"].at(n, 1))
                nc.vector.tensor_reduce(smx[:], mring_tile("s2")[:].rearrange("p (q t) -> p q t", q=QT), AX_X, ALU.max).then_inc(S["smx"].sem, 1)
                dve.wait_ge(S["smx"].sem, S["smx"].at(n, 1))
                nc.vector.tensor_scalar(snm[:], smx[:], -L1_SCALE, None, ALU.mult).then_inc(S["snm"].sem, 1)

            def s2_sum(n):
                dve.wait_ge(S["sp2"].sem, S["sp2"].at(n, QT))
                nc.vector.reciprocal(srec[:], ssum[:]).then_inc(S["srec"].sem, 1)

            def pv2(n):
                dve.wait_ge(S["pv2"].sem, S["pv2"].at(n, 1))
                dve.wait_ge(S["srec"].sem, S["srec"].at(n, 1))
                for q in range(QT):
                    nc.vector.scalar_tensor_tensor(out=t1[:, q, :], in0=mring_tile("pv2")[:, q * D:(q + 1) * D], scalar=srec[:, q:q + 1],
                                                   in1=bc[:, 6, :], op0=ALU.mult, op1=ALU.mult).then_inc(S["t1"].sem, 1)

            dve.wait_ge(s_small, 16 * N_SMALL)
            dve.wait_ge(s_bc, 2)
            run(dve, {"ms": meansq, "xn": xn, "T": transposed, "cT": ctx_transposed, "qk": qk, "pack": pack, "S": maxima, "maxsplit": maxsplit,
                      "at": normalise, "wo": wo, "gu": gu, "dn": dn, "lnstat": lnstat, "lncen": lncen, "sc": sc, "scn": scn, "s2": s2, "p2T": s2_sum, "pv2": pv2})

        @block.tensor
        def _(pe):
            mm = nc.tensor.matmul
            pe.wait_ge(s_small, 16 * N_SMALL)
            pe.wait_ge(s_vset, 10)
            for k in range(len(ROWS)):
                last = mm(ring[k // 4][:, (k // 2) % 2, (k % 2) * D:(k % 2 + 1) * D], ones_row, row_of(k), start=True, stop=True)
            last.then_inc(s_bcmm, 1)
            pe.wait_ge(s_bc, 2)
            pe.wait_ge(s_cset, 1 + 4 * PAIRS + 4)
            pe.wait_ge(s_wlo, len(W_ORDER))

            def exists(n):
                return not isinstance(n, int) or 0 <= n < B

            def last_fill(k, ahead, n):
                it = n - ahead[k]
                before = [(i, it) for i in range(k - 2, -1, -2)] + [(i, it - 1) for i in reversed(range(len(ahead))) if (i - k) % 2 == 0]
                for i, at0 in before:
                    if exists(at0 + ahead[i]):
                        return i, at0 + ahead[i]
                return None

            def fill(n, name):
                k = A_FILLS.index(name)
                before = last_fill(k, A_AHEAD, n)
                if before:
                    signal, j = freed(A_FILLS[before[0]])
                    pe.wait_ge(signal.sem, signal.at(before[1], j))
                return ring[k % 2]

            def mfill(n, name):
                k = M_FILLS.index(name)
                before = last_fill(k, M_AHEAD, n)
                if before:
                    signal, j = freed(M_FILLS[before[0]])
                    pe.wait_ge(signal.sem, signal.at(before[1], j))
                return mring[k % 2]

            def product(outs, left, right, chunks):
                total = len(PARTS) * chunks
                for k in range(total):
                    a, b = PARTS[k // chunks]
                    last = mm(outs, left(a, k % chunks), right(b, k % chunks), start=(k == 0), stop=(k == total - 1))
                return last

            def transposed(n, tag):
                pe.wait_ge(S[tag, "xn"].sem, S[tag, "xn"].at(n, QT))
                ps = mfill(n, "mT") if tag == "mlp" else fill(n, (tag, "T"))[:, 0, :]
                for c in range(C):
                    for q in range(QT):
                        last = nc.tensor.transpose(ps[:, c * T + q * P:c * T + (q + 1) * P], XN[tag][:, q, c * P:(c + 1) * P], ident[:])
                last.then_inc(S[tag, "T"].sem, 1)

            def ctx_transposed(n, tag):
                pe.wait_ge(c_in.sem, c_in.at(n, 16))
                ps = fill(n, ("ca", "cT"))
                for c in range(C):
                    last = nc.tensor.transpose(ps[:, 0, c * SKV:(c + 1) * SKV], ctx_sb[:, c * P:(c + 1) * P], ident[0:SKV, 0:SKV])
                last.then_inc(S["cTmm"].sem, 1)

            def qk(n, tag):
                pe.wait_ge(S[tag, "lo"].sem, S[tag, "lo"].at(n, C))
                if tag == "ca":
                    pe.wait_ge(S["cTlo"].sem, S["cTlo"].at(n, 1))
                ps = fill(n, (tag, "qk"))
                wq, wk = wt[f"{tag}_wq"], wt[f"{tag}_wk"]
                src, kw = (hT_a, T) if tag == "sa" else (cT, SKV2)
                for m in range(C):
                    product(ps[:, 0, m * T:(m + 1) * T], lambda a, kc: wq[a][:, kc, m * P:(m + 1) * P], lambda b, kc: hT_a[b][:, kc, :], C)
                for m in range(C):
                    last = product(ps[:, 1, m * kw:(m + 1) * kw], lambda a, kc: wk[a][:, kc, m * P:(m + 1) * P], lambda b, kc: src[b][:, kc, :], C)
                last.then_inc(S[tag, "qkmm"].sem, 1)

            def v(n, tag):
                ps = fill(n, (tag, "v"))
                wv = wt[f"{tag}_wv"]
                for q in range(QT if tag == "sa" else 1):
                    if tag == "sa":
                        last = product(ps[:, 0, q * D:(q + 1) * D], lambda a, kc: hT_a[a][:, kc, q * P:(q + 1) * P], lambda b, kc: wv[b][:, kc, :], C)
                    else:
                        last = product(ps[0:SKV, 0, 0:D], lambda a, kc: cT[a][:, kc, 0:SKV], lambda b, kc: wv[b][:, kc, :], C)
                last.then_inc(S[tag, "vmm"].sem, 1)

            def pack(n, tag, c):
                pe.wait_ge(S[tag, "qklo"].sem, S[tag, "qklo"].at(n, 2))
                ps = fill(n, (tag, "pq", c))
                for i in range(PAIRS):
                    for part in range(2):
                        last = mm(ps[:, i // 2, (i % 2) * T:(i % 2 + 1) * T], sel[:, part, i, :], qT[part][:, c, :], start=(part == 0), stop=(part == 1))
                last.then_inc(S[tag, "pqmm"].sem, 1)
                if tag == "sa":
                    ps = fill(n, (tag, "pk", c))
                    for i in range(PAIRS):
                        for part in range(2):
                            last = mm(ps[:, i // 2, (i % 2) * T:(i % 2 + 1) * T], sel[:, 2 + part, i, :], kT[part][:, c, :], start=(part == 0), stop=(part == 1))
                    last.then_inc(S[tag, "pkmm"].sem, 1)
                elif c == 0:
                    ps = fill(n, (tag, "pk", 0))
                    for cc in range(C):
                        for i in range(PAIRS):
                            for part in range(2):
                                last = mm(ps[:, cc, i * SKV2:(i + 1) * SKV2], sel[:, 2 + part, i, :], kT[part][:, cc, 0:SKV2], start=(part == 0), stop=(part == 1))
                    last.then_inc(S[tag, "pkmm"].sem, 1)

            def scores(n, tag, k):
                c, i0, pairs = pair_head(k, tag)
                if k == 0:
                    pe.wait_ge(S[tag, "pq"].sem, S[tag, "pq"].at(n, 2))
                    pe.wait_ge(S[tag, "pk"].sem, S[tag, "pk"].at(n, 4))
                ps = fill(n, (tag, "S", k))
                kw = T if tag == "sa" else SKV2
                for i in range(pairs):
                    for half in range(2):
                        for q in range(QT):
                            col = (i * QT + q) * kw
                            slot = PAIRS * c + i0 + i
                            last = mm(ps[:, half, col:col + kw], qpk[:, slot, q * P:(q + 1) * P], kpk[:, half, slot, 0:kw], start=True, stop=True)
                last.then_inc(S[tag, "S"].sem, 1)

            def maxT(n, tag, c):
                pe.wait_ge(S[tag, "nm"].sem, S[tag, "nm"].at(n, 4 * (c + 1)))
                ps = fill(n, (tag, "maxT", c))
                for q in range(QT):
                    last = nc.tensor.transpose(ps[0:80, 0, q * P:(q + 1) * P], nm[:, c, q, :], ident[:])
                last.then_inc(S[tag, "maxT"].sem, 1)

            def shifted(n, tag, k):
                c, kt, i0, g = shifted_at(k, tag)
                pe.wait_ge(S[tag, "maxrows"].sem, S[tag, "maxrows"].at(n, 2 * (c + 1)))
                ps = fill(n, (tag, "E", k))
                rows_ = P if tag == "sa" else SKV
                for half in range(2):
                    for u in range(2):
                        slot = PAIRS * c + i0 + u
                        last = mm(ps[0:rows_, half, u * T:(u + 1) * T], kpk[:, half, slot, kt * P:kt * P + rows_], qpk[:, slot, :], start=True, stop=True)
                last.then_inc(S[tag, "E"].sem, 1)

            def pv(n, tag, g):
                rows_, tiles = (P, QT) if tag == "sa" else (SKV, 1)
                c, kt = g // tiles, g % tiles
                pe.wait_ge(S[tag, "exp"].sem, S[tag, "exp"].at(n, 2 * (g + 1)))
                if g == 0:
                    pe.wait_ge(S[tag, "vz"].sem, S[tag, "vz"].at(n, 2))
                if kt == 0:
                    if c:
                        pe.wait_ge(S[tag, "at"].sem, S[tag, "at"].at(n, 1))
                    elif tag == "sa":
                        if not_first(n, 2):
                            pe.wait_ge(S["ca", "at"].sem, S["ca", "at"].at(n - 2, 2))
                    else:
                        pe.wait_ge(S["sa", "at"].sem, S["sa", "at"].at(sa_before_ca(n), 2))
                for half in range(2):
                    for what in range(2):
                        first = kt == 0 and half == 0 and what == 0
                        final = kt == tiles - 1 and half == 1
                        for i in range(PAIRS):
                            lhs = ones_pad[0:rows_, half, :] if what else vz[0:rows_, kt, 8 * c + 2 * i + half, :]
                            last = mm(od[32 * i:32 * i + 32, what, :], lhs, granule(g, tag)[0:rows_, i, half, :],
                                      start=first, stop=final, tile_position=(0, 32 * i), skip_group_check=True)
                last.then_inc(S[tag, "pv"].sem, 1)

            def wo(n, tag):
                pe.wait_ge(S[tag, "athi"].sem, S[tag, "athi"].at(n, 2))
                pe.wait_ge(S[tag, "atlo"].sem, S[tag, "atlo"].at(n, 2))
                ps = fill(n, (tag, "wo"))
                for q in range(QT):
                    last = product(ps[:, 0, q * D:(q + 1) * D], lambda a, kc: atT[a][:, kc, q * P:(q + 1) * P], lambda b, kc: wt[f"{tag}_wo"][b][:, kc, :], C)
                last.then_inc(S[tag, "wo"].sem, 1)

            def gu(n, m):
                if m == 0:
                    pe.wait_ge(S["mlp", "lo"].sem, S["mlp", "lo"].at(n, C))
                ps = mfill(n, f"gu{m}")
                for k, name in enumerate(("gate", "up")):
                    last = product(ps[:, k * T:(k + 1) * T], lambda a, kc: wt[name][a][:, kc, m * P:(m + 1) * P], lambda b, kc: hT_m[b][:, kc, :], C)
                last.then_inc(S["gu"].sem, 1)

            def dnp(n, m):
                pe.wait_ge(S["hidlo"].sem, S["hidlo"].at(n, m + 1))
                if m == 0 and not_first(n):
                    pe.wait_ge(S["h3"].sem, S["h3"].at(n - 1, 1))
                for q in range(QT):
                    for k, (a, b) in enumerate(PARTS):
                        last = mm(down_ps[:, q, :], hidT[a][:, m % HID, q * P:(q + 1) * P], wt["down"][b][:, m, :],
                                  start=(m == 0 and q == 0 and k == 0), stop=(m == M - 1 and k == len(PARTS) - 1), skip_group_check=True)
                last.then_inc(S["dnp"].sem, 1)

            def transposes(n, name, signal, src, tiles, rows_, cols):
                ps = mfill(n, name)
                for c in range(cols):
                    for q in range(tiles):
                        at0 = (c * tiles + q) * rows_
                        last = nc.tensor.transpose(ps[:, at0:at0 + rows_], src[:, q, c * P:(c + 1) * P], ident[0:rows_, 0:rows_])
                last.then_inc(S[signal].sem, 1)

            def t_nF(n):
                pe.wait_ge(S["nf", "nrm"].sem, S["nf", "nrm"].at(n, QT))
                transposes(n, "nFT", "nFTmm", nF, QT, P, C)

            def t_nX(n):
                pe.wait_ge(S["nx", "nrm"].sem, S["nx", "nrm"].at(n, 1))
                transposes(n, "nXT", "nXTmm", ctx_l, 1, SKV, C)

            def sc(n):
                pe.wait_ge(S["nFT"].sem, S["nFT"].at(n, 1))
                pe.wait_ge(S["nXT"].sem, S["nXT"].at(n, 1))
                ps = mfill(n, "sc")
                for q in range(QT):
                    for c in range(C):
                        mm(ps[:, q * SKV:(q + 1) * SKV], nFT[:, c, q * P:(q + 1) * P], nXT[:, c, :], start=(c == 0), stop=(c == C - 1))
                for c in range(C):
                    last = mm(ps[0:SKV, QT * SKV:QT * SKV + FC], nXT[:, c, :], fc1t_sb[:, c, :], start=(c == 0), stop=(c == C - 1))
                last.then_inc(S["scmm"].sem, 1)

            def pT(n):
                pe.wait_ge(S["lpn"].sem, S["lpn"].at(n, QT))
                ps = mfill(n, "pT")
                for q in range(QT):
                    last = nc.tensor.transpose(ps[0:SKV, q * P:(q + 1) * P], lp[:, q, :], ident[:])
                last.then_inc(S["pTmm"].sem, 1)

            def h4(n):
                pe.wait_ge(S["lpT"].sem, S["lpT"].at(n, 1))
                pe.wait_ge(S["xf"].sem, S["xf"].at(n, 1))
                ps = mfill(n, "h4")
                mm(ps[0:FC, 0:T], xf[:], lpT[:], start=True, stop=True).then_inc(S["h4"].sem, 1)

            def f2(n):
                pe.wait_ge(S["g5"].sem, S["g5"].at(n, 1))
                ps = mfill(n, "f2")
                for q in range(QT):
                    last = mm(ps[:, q * D:(q + 1) * D], g5[:, q * P:(q + 1) * P], fc2_sb[:], start=True, stop=True)
                last.then_inc(S["f2"].sem, 1)

            def t_nC(n):
                pe.wait_ge(S["nc", "nrm"].sem, S["nc", "nrm"].at(n, QT))
                transposes(n, "nCT", "nCTmm", nC, QT, P, C)

            def s2(n):
                pe.wait_ge(S["nCT"].sem, S["nCT"].at(n, 1))
                ps = mfill(n, "s2")
                for q in range(QT):
                    for c in range(C):
                        last = mm(ps[:, q * T:(q + 1) * T], nCT[:, c, q * P:(q + 1) * P], nCT[:, c, :], start=(c == 0), stop=(c == C - 1))
                last.then_inc(S["s2"].sem, 1)

            def t_p2(n):
                pe.wait_ge(S["sp2"].sem, S["sp2"].at(n, QT))
                transposes(n, "p2T", "p2Tmm", sp2, QT, P, QT)

            def pv2(n):
                pe.wait_ge(S["p2T"].sem, S["p2T"].at(n, 1))
                ps = mfill(n, "pv2")
                for q in range(QT):
                    for kt in range(QT):
                        last = mm(ps[:, q * D:(q + 1) * D], p2T[:, kt, q * P:(q + 1) * P], nC[:, kt, :], start=(kt == 0), stop=(kt == QT - 1))
                last.then_inc(S["pv2"].sem, 1)

            run(pe, {"T": transposed, "cT": ctx_transposed, "qk": qk, "v": v, "pack": pack, "S": scores, "maxT": maxT, "E": shifted,
                     "pv": pv, "wo": wo, "gu": gu, "dnp": dnp, "nFT": t_nF, "nXT": t_nX, "sc": sc, "pT": pT, "h4": h4, "f2": f2,
                     "nCT": t_nC, "s2": s2, "p2T": t_p2, "pv2": pv2})


def kernel(**inputs):
    import numpy as np
    import concourse.bacc as bacc
    from concourse.bass_utils import run_bass_kernel_spmd

    L0 = lambda n: np.ascontiguousarray(inputs[f"L0_xattn_{n}"])
    L1 = lambda n: np.ascontiguousarray(inputs[f"L1_xattn_{n}"])
    arrays = {
        "x": np.ascontiguousarray(inputs["x"]), "ctx": np.ascontiguousarray(inputs["ctx_1024"]),
        "vecs": np.stack([L1(n) for n in ("norm1_w", "norm1_b", "norm2_w", "norm2_b", "norm3_w", "norm3_b", "gamma1", "gamma2")]),
        "norm_w": np.ascontiguousarray(np.concatenate([L0(n).reshape(C, P) for n in ("sa_norm_w", "ca_norm_w", "mlp_norm_w")]).T),
        "fc1t": np.ascontiguousarray(L1("fc1_w").T), "fc1b": L1("fc1_b"),
        "fc2t": np.ascontiguousarray(L1("fc2_w").T), "fc2b": L1("fc2_b"),
    }
    names = {n: n for n in ATTN_W} | {"gate": "w_gate", "up": "w_up", "down": "w_down"}
    for n, m in names.items():
        arrays[f"w_{n}"] = L0(m)
    nc = bacc.Bacc("TRN2", target_bir_lowering=False, num_devices=1)
    ap = {n: nc.dram_tensor(n, a.shape, mybir.dt.from_np(a.dtype), kind="ExternalInput").ap() for n, a in arrays.items()}
    out = nc.dram_tensor("out", (B, T, D), F32, kind="ExternalOutput").ap()
    build(nc, ap["x"], ap["ctx"], {n: ap[f"w_{n}"] for n in names}, ap["vecs"], ap["norm_w"], ap["fc1t"], ap["fc1b"],
          ap["fc2t"], ap["fc2b"], out)
    r = run_bass_kernel_spmd(nc, [arrays], core_ids=[0])
    return r.results[0]["out"]
```
